# Optimizing a Trainium2 kernel written in Bass

```python
import numpy as np
import jax
import jax.numpy as jnp

def _softmax(x, axis=-1):
    return jax.nn.softmax(x, axis=axis)

def _gelu(x):
    return jax.nn.gelu(x, approximate=True)

def _silu(x):
    return jax.nn.silu(x)

def _sigmoid(x):
    return jax.nn.sigmoid(x)

def _layernorm(x, axis=-1, eps=1e-05):
    m = jnp.mean(x, axis=axis, keepdims=True)
    v = jnp.var(x, axis=axis, keepdims=True)
    return (x - m) / jnp.sqrt(v + eps)

def _scatter_add(tgt, idx, src, axis=0):
    return tgt.at[idx].add(src)

def _segment_sum(src, seg, n):
    return jax.ops.segment_sum(src, seg, n)
kernel_name = 'mk_prb_d1_jaxref_r8_4e994b'

def setup_inputs(seed: int=0):
    np.random.seed(seed)
    _w = jnp.asarray

    def _L0_attn_setup():
        import jax, jax.numpy as jnp
        import numpy as np
        DIM = 128
        HEADS = 16
        HEAD_DIM = DIM // HEADS

        def get_rope_matrix(seq_len: int, dim: int) -> jnp.ndarray:
            half = dim // 2
            inv_freq = 1.0 / 10000.0 ** (jnp.arange(half, dtype=jnp.float32) / half)
            sinusoid = jnp.arange(seq_len, dtype=jnp.float32)[:, None] * inv_freq[None, :]
            return jnp.concatenate([jnp.cos(sinusoid), jnp.sin(sinusoid)], axis=-1)
        key = jax.random.key(seed)
        ks = jax.random.split(key, 6)
        B, T, D = (2, 256, DIM)
        scale = 1.0 / np.sqrt(D)
        return {'x': jax.random.normal(ks[0], (B, T, D), dtype=jnp.float32), 'Wq': jax.random.normal(ks[1], (D, D), dtype=jnp.float32) * scale, 'Wk': jax.random.normal(ks[2], (D, D), dtype=jnp.float32) * scale, 'Wv': jax.random.normal(ks[3], (D, D), dtype=jnp.float32) * scale, 'Wo': jax.random.normal(ks[4], (D, D), dtype=jnp.float32) * scale, 'bo': jax.random.normal(ks[5], (D,), dtype=jnp.float32) * 0.01}
    _L0_attn_in = _L0_attn_setup()

    def _L0_ffn_setup():
        import jax, jax.numpy as jnp
        import numpy as np
        NUM_GEMMS = 8
        HIDDEN = 128
        INTER = 512
        key = jax.random.key(seed)
        k_x, k_w1, k_b1, k_w2, k_b2 = jax.random.split(key, 5)
        x = jax.random.normal(k_x, (8, 256, HIDDEN), dtype=jnp.float32)
        s1 = 1.0 / np.sqrt(HIDDEN)
        s2 = 1.0 / np.sqrt(INTER)
        W1 = jax.random.uniform(k_w1, (NUM_GEMMS, INTER, HIDDEN), jnp.float32, -s1, s1)
        b1 = jax.random.uniform(k_b1, (NUM_GEMMS, INTER), jnp.float32, -s1, s1)
        W2 = jax.random.uniform(k_w2, (NUM_GEMMS, HIDDEN, INTER), jnp.float32, -s2, s2)
        b2 = jax.random.uniform(k_b2, (NUM_GEMMS, HIDDEN), jnp.float32, -s2, s2)
        return {'x': x, 'W1': W1, 'b1': b1, 'W2': W2, 'b2': b2}
    _L0_ffn_in = _L0_ffn_setup()
    _d = {'L0_attn_x': _L0_attn_in['x'], 'L0_attn_Wq': _L0_attn_in['Wq'], 'L0_attn_Wk': _L0_attn_in['Wk'], 'L0_attn_Wv': _L0_attn_in['Wv'], 'L0_attn_Wo': _L0_attn_in['Wo'], 'L0_attn_bo': _L0_attn_in['bo'], 'L0_ffn_W1': _L0_ffn_in['W1'], 'L0_ffn_b1': _L0_ffn_in['b1'], 'L0_ffn_W2': _L0_ffn_in['W2'], 'L0_ffn_b2': _L0_ffn_in['b2']}
    _x0 = _d['L0_attn_x']
    _d['L0_attn_x'] = jax.random.normal(jax.random.fold_in(jax.random.key(seed), 1), (8, 512, 128), dtype=_x0.dtype)
    del _x0
    return _d

def reference(L0_attn_x, L0_attn_Wq, L0_attn_Wk, L0_attn_Wv, L0_attn_Wo, L0_attn_bo, L0_ffn_W1, L0_ffn_b1, L0_ffn_W2, L0_ffn_b2):

    def _L0_attn_ref(x, Wq, Wk, Wv, Wo, bo):
        import jax, jax.numpy as jnp
        import numpy as np
        DIM = 128
        HEADS = 16
        HEAD_DIM = DIM // HEADS

        def get_rope_matrix(seq_len: int, dim: int) -> jnp.ndarray:
            half = dim // 2
            inv_freq = 1.0 / 10000.0 ** (jnp.arange(half, dtype=jnp.float32) / half)
            sinusoid = jnp.arange(seq_len, dtype=jnp.float32)[:, None] * inv_freq[None, :]
            return jnp.concatenate([jnp.cos(sinusoid), jnp.sin(sinusoid)], axis=-1)
        B, T, D = x.shape
        H, hd = (HEADS, HEAD_DIM)

        def split_heads(y):
            return y.reshape(B, T, H, hd).transpose(0, 2, 1, 3)
        q = split_heads(x @ Wq)
        k = split_heads(x @ Wk)
        v = split_heads(x @ Wv)
        rope = get_rope_matrix(T, hd)
        v_r = jnp.einsum('bhnd,sd->bhns', v, rope)
        scores = jax.nn.softmax(jnp.einsum('bhnd,bhmd->bhnm', q, k) / jnp.sqrt(jnp.float32(hd)), axis=-1)
        out = jnp.einsum('bhnm,bhms->bhns', scores, v_r)
        out = jnp.einsum('bhnt,ts->bhns', out, rope)
        out = out.transpose(0, 2, 1, 3).reshape(B, T, D)
        return out @ Wo + bo

    def _L0_ffn_ref(x, W1, b1, W2, b2):
        import jax, jax.numpy as jnp
        import numpy as np
        NUM_GEMMS = 8
        HIDDEN = 128
        INTER = 512
        orig_shape = x.shape
        token_num = int(np.prod(orig_shape[:-1]))
        m = token_num // NUM_GEMMS
        xg = x.reshape(NUM_GEMMS, m, HIDDEN)
        h1 = jnp.einsum('gmh,goh->gmo', xg, W1) + b1[:, None, :]
        h2 = jnp.einsum('gmo,gho->gmh', h1, W2) + b2[:, None, :]
        return h2.reshape(orig_shape)
    x = L0_attn_x
    xn = _layernorm(x, axis=-1)
    x = x + _L0_attn_ref(xn, L0_attn_Wq, L0_attn_Wk, L0_attn_Wv, L0_attn_Wo, L0_attn_bo) + _L0_ffn_ref(xn, L0_ffn_W1, L0_ffn_b1, L0_ffn_W2, L0_ffn_b2)
    return x

_drawn_inputs = setup_inputs


def setup_inputs(seed=0):
    import zlib

    import numpy as np

    out = dict(_drawn_inputs(seed))
    spreads = {}
    factors = {'L0_attn_bo': 64.0,
     'L0_ffn_W1': 5.414,
     'L0_ffn_b1': 8.0,
     'L0_ffn_W2': 5.129,
     'L0_ffn_b2': 64.0}
    for name, (base, spread) in spreads.items():
        noise = np.random.default_rng([zlib.crc32(name.encode()), seed]).standard_normal(out[name].shape)
        drawn = base * np.exp(spread * noise) if base else spread * noise
        out[name] = jnp.asarray(drawn.astype(out[name].dtype))
    for name, factor in factors.items():
        out[name] = (out[name] * factor).astype(out[name].dtype)
    return out
```

```python
from contextlib import ExitStack

import numpy as np

import concourse.bass as bass
from concourse import mybir

F32 = mybir.dt.float32
BF16 = mybir.dt.bfloat16
ALU = mybir.AluOpType
ACT = mybir.ActivationFunctionType
AX_X = mybir.AxisListType.X

P = 128
B, T, D = 8, 512, 128
H, HD = 16, 8
C = T // P
GH = 4
NG = H // GH
FC = 512 // P
NP3 = 3
ROWS = NP3 * NP3 * HD
QROWS = ROWS + NP3
EPS = 1e-5
ONES_PAIR = float(np.array([0x3F803F80], np.uint32).view(np.float32)[0])

PROLOGUE = ["xnT", "q", "k", "v", "gram", "wo2", "b1T", "w2T", "w12", "ffn", "max"]
MIDDLE = ["max0", "xnT", "q", "k", "max1", "v", "w2T", "w12", "ffn", "max2", "max3", "out"]
FIRST = MIDDLE[:-1]
LAST = ["max0", "max1", "max2", "out"]


def turn(b, kind, job):
    if kind == "prologue":
        return PROLOGUE.index(job)
    if kind == "first":
        return len(PROLOGUE) + FIRST.index(job)
    jobs = {"middle": MIDDLE, "last": LAST}[kind]
    return b * len(MIDDLE) + (len(PROLOGUE) + len(FIRST) - len(MIDDLE) + jobs.index(job))


def build(nc, x, wq, wk, wv, wo, bo, w1, b1, w2, b2, rope16, headmask, identity, out):
    with ExitStack() as ctx:
        def sb(name, shape, dt):
            return ctx.enter_context(nc.sbuf_tensor(name, shape, dt))

        def sem(name):
            return ctx.enter_context(nc.semaphore(name))

        ident = sb("ident", [P, P], F32)
        rope_sb = sb("rope_sb", [P, C, P], F32)
        mask_sb = sb("mask_sb", [P, P], F32)
        gram = sb("gram", [P, P], F32)
        wq_sb = sb("wq_sb", [P, D], F32)
        wk_sb = sb("wk_sb", [P, D], F32)
        wv_sb = sb("wv_sb", [P, D], F32)
        wo_sb = sb("wo_sb", [P, D], F32)
        wo2 = sb("wo2", [P, D], F32)
        w1_sb = sb("w1_sb", [P, FC, D], F32)
        w2_sb = sb("w2_sb", [P, FC * P], F32)
        w2T = sb("w2T", [P, FC, D], F32)
        w12 = sb("w12", [P, D], F32)
        b1_rows = sb("b1_rows", [B * FC, P], F32)
        b1T = sb("b1T", [P, B * FC], F32)
        b1_now = sb("b1_now", [P, FC], F32)
        b2_all = sb("b2_all", [P, B * D], F32)
        bo_all = sb("bo_all", [P, D], F32)
        bias = sb("bias", [P, D], F32)
        x_all = sb("x_all", [P, B * C * D], F32)
        stats = sb("stats", [P, B * C, 6], F32)
        mv = sb("mv", [P, B * C, 2], F32)
        rstd = sb("rstd", [P, B * C], F32)
        half = sb("half", [P, B * C], F32)
        xn = sb("xn", [P, C, D], F32)
        xnT = sb("xnT", [P, T], F32)
        qk_f = sb("qk_f", [P, 2, T], F32)
        qk_r = sb("qk_r", [P, 2, T], F32)
        parts = sb("parts", [P, 2, NP3, T], BF16)
        zero_rows = sb("zero_rows", [H, NP3 * T], BF16)
        q_stack = sb("q_stack", [P, NG, GH, T], BF16)
        k_stack = sb("k_stack", [P, NG, GH, T], BF16)
        v_stage = sb("v_stage", [P, C, H, HD], F32)
        v_ones = sb("v_ones", [P, C, H, 32], F32)
        negmax = sb("negmax", [P, 2, GH * C], F32)
        max_f = sb("max_f", [GH * C, P], F32)
        max_r = sb("max_r", [GH * C, P], F32)
        max_parts = sb("max_parts", [GH * C, NP3, P], BF16)
        probs = sb("probs", [P, 2, GH, C, T], F32)
        u_sb = sb("u_sb", [P, NG, T], F32)
        heads = sb("heads", [P, T], F32)
        den = sb("den", [P, T // HD], F32)
        rden = sb("rden", [P, T // HD], F32)
        rden_all = sb("rden_all", [P, T], F32)
        headsn = sb("headsn", [P, T], F32)
        y_base = sb("y_base", [P, B * C * D], F32)
        y = sb("y", [P, C, D], F32)

        q_dram = nc.dram_tensor("q_scratch", [H, QROWS, T], BF16).ap()
        k_dram = nc.dram_tensor("k_scratch", [H, NP3, HD, T], BF16).ap()
        u_dram = nc.dram_tensor("u_scratch", [H, HD + 1, T], F32).ap()
        r_dram = nc.dram_tensor("r_scratch", [H, T], F32).ap()

        ps_m = ctx.enter_context(nc.psum_tensor("ps_m", [P, 4, T], F32))
        ps_e = ctx.enter_context(nc.psum_tensor("ps_e", [P, 2, T], F32))
        ps_u = ctx.enter_context(nc.psum_tensor("ps_u", [P, T], F32))
        ps_side = ctx.enter_context(nc.psum_tensor("ps_side", [P, T], F32))

        x0_in, x_in, wqkv_in, ffn_in, const_in, bias_in = map(
            sem, ["x0_in", "x_in", "wqkv_in", "ffn_in", "const_in", "bias_in"])
        filled, cleared = sem("filled"), sem("cleared")
        zeros_out = sem("zeros_out")
        ln_stat, ln_rstd, xn_ready = map(sem, ["ln_stat", "ln_rstd", "xn_ready"])
        gram_ready = sem("gram_ready")
        side_mm, side_evac = sem("side_mm"), sem("side_evac")
        qk_split, scratch_w = sem("qk_split"), sem("scratch_w")
        stack_in = [sem(f"stack_in{g}") for g in range(NG)]
        v_copied = sem("v_copied")
        b1_copied = sem("b1_copied")
        bias_done, base_done = sem("bias_done"), sem("base_done")
        m_ready, m_done, max_split = map(sem, ["m_ready", "m_done", "max_split"])
        max_in = [sem(f"max_in{g}") for g in range(NG)]
        e_ready, e_done, pv_done, u_done = map(sem, ["e_ready", "e_done", "pv_done", "u_done"])
        u_out = [sem(f"u_out{g}") for g in range(NG)]
        heads_in, den_in, rden_done, rden_out, rden_in, norm_done = map(
            sem, ["heads_in", "den_in", "rden_done", "rden_out", "rden_in", "norm_done"])
        y_out = sem("y_out")

        block = ctx.enter_context(nc.Block())

        def previous(b, kind, job):
            if kind == "first":
                return turn(0, "prologue", job)
            if kind == "second":
                return turn(0, "first", job)
            return turn(b - 1, "middle", job)

        @block.tensor
        def _(pe):
            def side(index):
                if isinstance(index, int) and index == 0:
                    return
                pe.wait_ge(side_evac, index)

            def transpose4(src):
                for c in range(4):
                    last = nc.tensor.transpose(ps_side[:, c * P:(c + 1) * P], src(c), ident[:, :])
                last.then_inc(side_mm, 1)

            def job_xnT(b, index):
                side(index)
                pe.wait_ge(xn_ready, 4 * b + 4)
                transpose4(lambda c: xn[:, c, :])

            def job_q(index):
                side(index)
                nc.tensor.matmul(ps_side[:, :], wq_sb[:, :], xnT[:, :], start=True, stop=True).then_inc(side_mm, 1)

            def job_k(index):
                side(index)
                nc.tensor.matmul(ps_side[:, :], wk_sb[:, :], xnT[:, :], start=True, stop=True).then_inc(side_mm, 1)

            def job_v(index):
                side(index)
                for c in range(C):
                    last = nc.tensor.matmul(ps_side[:, c * D:(c + 1) * D], xnT[:, c * P:(c + 1) * P], wv_sb[:, :],
                                            start=True, stop=True)
                last.then_inc(side_mm, 1)

            def job_w2T(b, index):
                side(index)
                pe.wait_ge(ffn_in, 32 * b + 32)
                transpose4(lambda c: w2_sb[:, c * P:(c + 1) * P])

            def job_w12(b, index):
                side(index)
                for c in range(FC):
                    nc.tensor.matmul(ps_side[:, 0:D], w1_sb[:, c, :], w2T[:, c, :], start=(c == 0), stop=(c == FC - 1))
                pe.wait_ge(b1_copied, b + 1)
                for c in range(FC):
                    last = nc.tensor.matmul(ps_side[:, D:2 * D], b1_now[:, c:c + 1].to_broadcast([P, P]), w2T[:, c, :],
                                            start=(c == 0), stop=(c == FC - 1))
                last.then_inc(side_mm, 1)

            def job_ffn(index):
                side(index)
                for c in range(C):
                    last = nc.tensor.matmul(ps_side[:, c * D:(c + 1) * D], xnT[:, c * P:(c + 1) * P], w12[:, :],
                                            start=True, stop=True)
                last.then_inc(side_mm, 1)

            def job_max(G, parity, index):
                side(index)
                pe.wait_ge(m_done, 8 * G + 8)
                nc.tensor.transpose(ps_side[0:GH * C, 0:P], negmax[:, parity, :], ident[:, :]).then_inc(side_mm, 1)

            def job_out(b, index):
                side(index)
                pe.wait_ge(norm_done, b + 1)
                for c in range(C):
                    last = nc.tensor.matmul(ps_side[:, c * D:(c + 1) * D], headsn[:, c * P:(c + 1) * P], wo2[:, :],
                                            start=True, stop=True)
                last.then_inc(side_mm, 1)

            def m_tile(G, g, i, c):
                pair = 8 * G + (2 * i + c // 2)
                if i == 0 and c == 0 and not isinstance(G, int):
                    pass
                if c % 2 == 0 and not (isinstance(pair, int) and pair < 2):
                    pe.wait_ge(m_done, pair - 1)
                mm = nc.tensor.matmul(ps_m[:, 2 * ((c // 2) % 2) + c % 2, :], q_stack[:, g, i, c * P:(c + 1) * P],
                                      k_stack[:, g, i, :], start=True, stop=True)
                if c % 2:
                    mm.then_inc(m_ready, 1)

            def e_tile(G, g, i, c):
                tile = 16 * G + (4 * i + c)
                if not (isinstance(tile, int) and tile < 2):
                    pe.wait_ge(e_done, tile - 1)
                nc.tensor.matmul(ps_e[:, c % 2, :], k_stack[:, g, i, c * P:(c + 1) * P], q_stack[:, g, i, :],
                                 start=True, stop=True).then_inc(e_ready, 1)

            def pv_chunk(G, g, c):
                if c == 0:
                    pe.wait_ge(e_done, 16 * G + 16)
                    if not (isinstance(G, int) and G == 0):
                        pe.wait_ge(u_done, G)
                for j in range(GH):
                    last = nc.tensor.matmul(ps_u[32 * j:32 * j + 32, :], v_ones[:, c, GH * g + j, :],
                                            probs[:, g % 2, j, c, :], start=(c == 0), stop=(c == C - 1))
                last.then_inc(pv_done, 1)

            def step(b, s, kind, jobs):
                G = 4 * b + s
                do_m = kind != "last" or s < 2
                do_pv = not (kind == "first" and s == 0)
                g_m = (s + 2) % NG
                b_m = b if s < 2 else b + 1
                for i in range(GH):
                    if i == 0:
                        pe.wait_ge(max_in[s], 48 * b + 48)
                        if do_m:
                            pe.wait_ge(stack_in[g_m], 64 * b_m + 64)
                    for c in range(2):
                        e_tile(G, s, i, c)
                        if do_m:
                            m_tile(G + 2, g_m, i, c)
                    if (i, 0) in jobs:
                        jobs[i, 0]()
                    if do_pv:
                        if s == 1 and i == 0:
                            pe.wait_ge(v_copied, 4 * b + 4)
                        pv_chunk(G - 1, (s - 1) % NG, i)
                    for c in range(2, 4):
                        e_tile(G, s, i, c)
                        if do_m:
                            m_tile(G + 2, g_m, i, c)
                    if (i, 1) in jobs:
                        jobs[i, 1]()

            def batch(b, kind):
                t = lambda job: turn(b, kind, job)
                step(b, 0, kind, {(0, 0): lambda: job_max(4 * b + 1, 1, t("max0"))} | ({} if kind == "last" else {
                    (0, 1): lambda: job_xnT(b + 1, t("xnT")),
                    (1, 0): lambda: job_q(t("q")),
                    (1, 1): lambda: job_k(t("k"))}))
                step(b, 1, kind, {(0, 0): lambda: job_max(4 * b + 2, 0, t("max1"))} | ({} if kind == "last" else {
                    (1, 0): lambda: job_v(t("v")),
                    (1, 1): lambda: job_w2T(b + 1, t("w2T")),
                    (2, 1): lambda: job_w12(b + 1, t("w12")),
                    (3, 1): lambda: job_ffn(t("ffn"))}))
                step(b, 2, kind, {(0, 0): lambda: job_max(4 * b + 3, 1, t("max2"))})
                jobs = {}
                if kind != "last":
                    jobs[0, 0] = lambda: job_max(4 * b + 4, 0, t("max3"))
                if kind != "first":
                    jobs[2, 0] = lambda: job_out(b - 1, t("out"))
                step(b, 3, kind, jobs)

            t = lambda job: turn(0, "prologue", job)
            pe.wait_ge(const_in, 16)
            job_xnT(0, t("xnT"))
            pe.wait_ge(wqkv_in, 48)
            job_q(t("q"))
            job_k(t("k"))
            job_v(t("v"))
            side(t("gram"))
            pe.wait_ge(const_in, 64)
            for c in range(C):
                last = nc.tensor.matmul(ps_side[:, 0:P], rope_sb[:, c, :], rope_sb[:, c, :],
                                        start=(c == 0), stop=(c == C - 1))
            last.then_inc(side_mm, 1)
            side(t("wo2"))
            nc.tensor.matmul(ps_side[:, 0:D], gram[:, :], wo_sb[:, :], start=True, stop=True).then_inc(side_mm, 1)
            side(t("b1T"))
            pe.wait_ge(bias_in, 48)
            nc.tensor.transpose(ps_side[:, 0:B * FC], b1_rows[:, :], ident[0:B * FC, 0:B * FC]).then_inc(side_mm, 1)
            job_w2T(0, t("w2T"))
            job_w12(0, t("w12"))
            job_ffn(t("ffn"))
            for G in range(2):
                pe.wait_ge(stack_in[G], 64)
                for i in range(GH):
                    for c in range(C):
                        m_tile(G, G, i, c)
                    if G == 1 and i == 1:
                        job_max(0, 0, t("max"))
            batch(0, "first")
            with pe.Fori(1, B - 1) as b:
                batch(b, "middle")
            batch(B - 1, "last")
            for c in range(C):
                pv_chunk(4 * B - 1, NG - 1, c)
            job_out(B - 1, turn(B - 1, "last", "out") + 1)

        @block.scalar
        def _(act):
            def evac(index, pairs):
                act.wait_ge(side_mm, index + 1)
                for dst, src in pairs:
                    last = nc.scalar.activation(dst, src, ACT.Copy)
                last.then_inc(side_evac, 1)

            def evac_qk(b, index, o):
                if not (isinstance(b, int) and b == 0):
                    act.wait_ge(scratch_w, 192 * b)
                evac(index, [(qk_f[:, o, :], ps_side[:, :]), (parts[:, o, 0, :], ps_side[:, :])])

            def evac_v(b, index):
                evac(index, [(v_stage[:, :, :, :].rearrange("p c h d -> p (c h d)"), ps_side[:, :])])

            def copy_v(c):
                nc.scalar.activation(v_ones[:, c, :, 0:HD], v_stage[:, c, :, :], ACT.Copy).then_inc(v_copied, 1)

            def evac_max(b, s, index):
                if not (isinstance(b, int) and b == 0 and s == 0):
                    before = b if s > 0 else b - 1
                    act.wait_ge(max_in[(s - 1) % NG], 48 * before + 48)
                evac(index, [(max_f[:, :], ps_side[0:GH * C, 0:P]), (max_parts[:, 0, :], ps_side[0:GH * C, 0:P])])

            def evac_u(b, G, g):
                act.wait_ge(pv_done, 4 * G + 4)
                if not (isinstance(b, int) and b == 0):
                    act.wait_ge(u_out[g], 64 * b)
                nc.scalar.activation(u_sb[:, g, :], ps_u[:, :], ACT.Copy).then_inc(u_done, 1)

            def step(b, s, kind, jobs):
                G = 4 * b + s
                for i in range(GH):
                    for c in range(C):
                        if c == 2:
                            if s == 0 and kind != "first":
                                act.wait_ge(pv_done, 16 * b + (i - 3))
                                copy_v(i)
                            if (i, 0) in jobs:
                                jobs[i, 0]()
                            if i == GH - 1 and not (kind == "first" and s == 0):
                                evac_u(b if s > 0 else b - 1, G - 1, (s - 1) % NG)
                        act.wait_ge(e_ready, 16 * G + (4 * i + c + 1))
                        nc.scalar.activation(probs[:, s % 2, i, c, :], ps_e[:, c % 2, :], ACT.Exp,
                                             scale=float(HD) ** -0.5).then_inc(e_done, 1)
                    if (i, 1) in jobs:
                        jobs[i, 1]()

            def batch(b, kind):
                t = lambda job: turn(b, kind, job)
                flat = xnT[:, :]
                step(b, 0, kind, {(0, 0): lambda: evac_max(b, 1, t("max0"))} | ({} if kind == "last" else {
                    (0, 1): lambda: evac(t("xnT"), [(flat, ps_side[:, :])]),
                    (1, 0): lambda: evac_qk(b + 1, t("q"), 0),
                    (1, 1): lambda: evac_qk(b + 1, t("k"), 1)}))
                step(b, 1, kind, {(0, 0): lambda: evac_max(b, 2, t("max1"))} | ({} if kind == "last" else {
                    (1, 0): lambda: evac_v(b + 1, t("v")),
                    (1, 1): lambda: evac(t("w2T"), [(w2T[:, :, :].rearrange("p c h -> p (c h)"), ps_side[:, :])]),
                    }))
                step(b, 2, kind, {(0, 0): lambda: evac_max(b, 3, t("max2"))})
                step(b, 3, kind, {} if kind == "last" else {(0, 0): lambda: evac_max(b + 1, 0, t("max3"))})

            t = lambda job: turn(0, "prologue", job)
            evac(t("xnT"), [(xnT[:, :], ps_side[:, :])])
            evac_qk(0, t("q"), 0)
            evac_qk(0, t("k"), 1)
            evac_v(0, t("v"))
            act.wait_ge(filled, 3)
            act.wait_ge(side_evac, t("v") + 1)
            for c in range(C):
                copy_v(c)
            evac(t("wo2"), [(wo2[:, :], ps_side[:, 0:D])])
            evac(t("b1T"), [(b1T[:, :], ps_side[:, 0:B * FC])])
            evac(t("w2T"), [(w2T[:, :, :].rearrange("p c h -> p (c h)"), ps_side[:, :])])
            evac_max(0, 0, t("max"))
            batch(0, "first")
            with act.Fori(1, B - 1) as b:
                batch(b, "middle")
            batch(B - 1, "last")
            evac_u(B - 1, 4 * B - 1, NG - 1)

        @block.vector
        def _(dve):
            def stat(c0, c1):
                for c in range(c0, c1):
                    last = nc.vector.bn_stats(stats[:, c, :], x_all[:, c * D:(c + 1) * D])
                last.then_inc(ln_stat, 1)

            def aggregate(c0, c1, count):
                dve.wait_ge(ln_stat, count)
                for c in range(c0, c1):
                    last = nc.vector.bn_aggr(mv[:, c, :], stats[:, c, :])
                last.then_inc(ln_stat, 1)

            def normalise(b, kind):
                if kind is not None:
                    dve.wait_ge(side_mm, previous(b, kind, "xnT") + 1)
                for c in range(C):
                    col = b * C + c
                    nc.vector.tensor_scalar(xn[:, c, :], x_all[:, bass.ds(b * (C * D) + c * D, D)],
                                            mv[:, bass.ds(col, 1), 0], rstd[:, bass.ds(col, 1)],
                                            ALU.subtract, ALU.mult).then_inc(xn_ready, 1)

            def reduce_pair(G, parity, i, h):
                dve.wait_ge(m_ready, 8 * G + (2 * i + h + 1))
                nc.vector.tensor_reduce(negmax[:, parity, C * i + 2 * h:C * i + 2 * h + 2], ps_m[:, 2 * h:2 * h + 2, :],
                                        AX_X, ALU.max, negate=True).then_inc(m_done, 1)

            def reciprocals(b):
                dve.wait_ge(den_in, 16 * b + 16)
                if not (isinstance(b, int) and b == 0):
                    dve.wait_ge(rden_out, 16 * b)
                nc.vector.reciprocal(rden[:, :], den[:, :]).then_inc(rden_done, 1)

            def finish(b, index):
                dve.wait_ge(side_mm, index + 1)
                if not (isinstance(b, int) and b == 0):
                    dve.wait_ge(y_out, 16 * b)
                nc.vector.tensor_tensor(y[:, :, :].rearrange("p c d -> p (c d)"), ps_side[:, :],
                                        y_base[:, bass.ds(b * (C * D), C * D)], ALU.add).then_inc(side_evac, 1)

            def evac_w12(b, index):
                dve.wait_ge(side_mm, index + 1)
                nc.vector.tensor_copy(w12[:, :], ps_side[:, 0:D])
                nc.vector.tensor_tensor(bias[:, :], ps_side[:, D:2 * D], b2_all[:, bass.ds(b * D, D)],
                                        ALU.add).then_inc(side_evac, 1)

            def evac_ffn(b, index):
                rows = y_base[:, bass.ds(b * (C * D), C * D)]
                dve.wait_ge(side_mm, index + 1)
                nc.vector.tensor_tensor(rows, ps_side[:, :], x_all[:, bass.ds(b * (C * D), C * D)],
                                        ALU.add).then_inc(side_evac, 1)
                dve.wait_ge(side_evac, index + 1)
                rows4 = rows.rearrange("p (c d) -> p c d", c=C)
                nc.vector.tensor_tensor(rows4, rows4, bias[:, :].rearrange("p (o d) -> p o d", o=1).to_broadcast([P, C, D]),
                                        ALU.add).then_inc(base_done, 1)

            def step(b, s, kind, jobs):
                G = 4 * b + s
                do_m = kind != "last" or s < 2
                for i in range(GH):
                    for h in range(2):
                        if do_m:
                            reduce_pair(G + 2, s % 2, i, h)
                        if (i, h) in jobs:
                            jobs[i, h]()

            def batch(b, kind):
                if kind != "last":
                    if kind == "first":
                        normalise(1, "first")
                    else:
                        dve.wait_ge(side_mm, b * len(MIDDLE) + (len(PROLOGUE) - 1 - len(MIDDLE) + MIDDLE.index("xnT") + 1))
                        for c in range(C):
                            nc.vector.tensor_scalar(xn[:, c, :], x_all[:, bass.ds(b * (C * D) + (C + c) * D, D)],
                                                    mv[:, bass.ds(b * C + (C + c), 1), 0],
                                                    rstd[:, bass.ds(b * C + (C + c), 1)],
                                                    ALU.subtract, ALU.mult).then_inc(xn_ready, 1)
                step(b, 0, kind, {})
                t = lambda job: turn(b, kind, job)
                step(b, 1, kind, ({} if kind == "first" else {(3, 0): lambda: reciprocals(b - 1)}) |
                     ({} if kind == "last" else {(2, 1): lambda: evac_w12(b + 1, t("w12")),
                                                 (3, 1): lambda: evac_ffn(b + 1, t("ffn"))}))
                step(b, 2, kind, {})
                step(b, 3, kind, {} if kind == "first" else {
                    (2, 0): lambda: finish(b - 1, turn(b, kind, "out"))})

            nc.vector.memset(half[:, :], -0.5).then_inc(cleared, 1)
            nc.vector.memset(q_stack[64:P, :, :, :].rearrange("p g i t -> p (g i t)").bitcast(F32), 0.0).then_inc(cleared, 1)
            dve.wait_ge(x0_in, 16)
            stat(0, C)
            aggregate(0, C, 1)
            dve.wait_ge(ln_rstd, 2)
            normalise(0, None)
            dve.wait_ge(x_in, 16)
            stat(C, B * C)
            aggregate(C, B * C, 3)
            dve.wait_ge(side_mm, turn(0, "prologue", "gram") + 1)
            dve.wait_ge(const_in, 64)
            nc.vector.tensor_tensor(gram[:, :], ps_side[:, 0:P], mask_sb[:, :], ALU.mult).then_inc(side_evac, 1)
            dve.wait_ge(bias_in, 48)
            nc.vector.tensor_tensor(b2_all[:, :].rearrange("p (g d) -> p g d", g=B), b2_all[:, :].rearrange("p (g d) -> p g d", g=B),
                                    bo_all[:, :].rearrange("p (o d) -> p o d", o=1).to_broadcast([P, B, D]),
                                    ALU.add).then_inc(bias_done, 1)
            dve.wait_ge(bias_done, 1)
            evac_w12(0, turn(0, "prologue", "w12"))
            evac_ffn(0, turn(0, "prologue", "ffn"))
            dve.wait_ge(ln_rstd, 4)
            for G in range(2):
                for i in range(GH):
                    for h in range(2):
                        reduce_pair(G, G, i, h)
            batch(0, "first")
            with dve.Fori(1, B - 1) as b:
                batch(b, "middle")
            batch(B - 1, "last")
            reciprocals(B - 1)
            finish(B - 1, turn(B - 1, "last", "out") + 1)

        @block.gpsimd
        def _(pool):
            def split_qk(b, index, o):
                pool.wait_ge(side_evac, index + 1)
                nc.gpsimd.tensor_tensor(parts[:, o, 1, :], qk_f[:, o, :], parts[:, o, 0, :],
                                        ALU.subtract).then_inc(qk_split, 1)
                nc.gpsimd.tensor_tensor(qk_r[:, o, :], qk_f[:, o, :], parts[:, o, 0, :],
                                        ALU.subtract).then_inc(qk_split, 1)
                pool.wait_ge(qk_split, 6 * b + (3 * o + 2))
                nc.gpsimd.tensor_tensor(parts[:, o, 2, :], qk_r[:, o, :], parts[:, o, 1, :],
                                        ALU.subtract).then_inc(qk_split, 1)

            def split_max(G, index):
                pool.wait_ge(side_evac, index + 1)
                nc.gpsimd.tensor_tensor(max_parts[:, 1, :], max_f[:, :], max_parts[:, 0, :],
                                        ALU.subtract).then_inc(max_split, 1)
                nc.gpsimd.tensor_tensor(max_r[:, :], max_f[:, :], max_parts[:, 0, :],
                                        ALU.subtract).then_inc(max_split, 1)
                pool.wait_ge(max_split, 3 * G + 2)
                nc.gpsimd.tensor_tensor(max_parts[:, 2, :], max_r[:, :], max_parts[:, 1, :],
                                        ALU.subtract).then_inc(max_split, 1)

            def copy_b1(b):
                nc.gpsimd.tensor_copy(b1_now[:, :], b1T[:, bass.ds(b * FC, FC)]).then_inc(b1_copied, 1)

            def norm(b):
                pool.wait_ge(heads_in, 16 * b + 16)
                pool.wait_ge(rden_in, 16 * b + 16)
                nc.gpsimd.tensor_tensor(headsn[:, :], heads[:, :], rden_all[:, :], ALU.mult).then_inc(norm_done, 1)

            def batch(b, kind):
                t = lambda job: turn(b, kind, job)
                split_max(4 * b + 1, t("max0"))
                if kind != "last":
                    split_qk(b + 1, t("q"), 0)
                    split_qk(b + 1, t("k"), 1)
                    copy_b1(b + 1)
                split_max(4 * b + 2, t("max1"))
                split_max(4 * b + 3, t("max2"))
                if kind != "last":
                    split_max(4 * b + 4, t("max3"))
                if kind != "first":
                    norm(b - 1)

            nc.gpsimd.memset(zero_rows[:, :], 0.0).then_inc(filled, 1)
            nc.gpsimd.memset(v_ones[:, :, :, :], 1.0).then_inc(filled, 1)
            pool.wait_ge(filled, 2)
            nc.gpsimd.memset(k_stack[64:P, :, :, :].rearrange("p g i t -> p (g i t)").bitcast(F32),
                             ONES_PAIR).then_inc(filled, 1)

            def inverse_std(c0, c1, stat_count, rstd_count):
                pool.wait_ge(ln_stat, stat_count)
                nc.gpsimd.tensor_scalar(rstd[:, c0:c1], mv[:, c0:c1, 1], 1.0, EPS, ALU.mult, ALU.add).then_inc(ln_rstd, 1)
                pool.wait_ge(ln_rstd, rstd_count)
                nc.gpsimd.tensor_tensor(rstd[:, c0:c1], rstd[:, c0:c1], half[:, c0:c1], ALU.pow).then_inc(ln_rstd, 1)

            pool.wait_ge(cleared, 1)
            pool.wait_ge(filled, 3)
            inverse_std(0, C, 2, 1)
            t = lambda job: turn(0, "prologue", job)
            split_qk(0, t("q"), 0)
            split_qk(0, t("k"), 1)
            inverse_std(C, B * C, 4, 3)
            pool.wait_ge(side_evac, t("b1T") + 1)
            copy_b1(0)
            split_max(0, t("max"))
            batch(0, "first")
            with pool.Fori(1, B - 1) as b:
                batch(b, "middle")
            batch(B - 1, "last")
            pool.wait_ge(side_mm, turn(B - 1, "last", "out") + 1)
            norm(B - 1)

        @block.sync
        def _(sp):
            def load_stack(g, b):
                hs = slice(GH * g, GH * g + GH)
                sp.dma_start(q_stack[0:QROWS, g, :, :], q_dram[hs, :, :].rearrange("h r t -> r h t")).then_inc(stack_in[g], 16)
                for a in range(NP3):
                    sp.dma_start(k_stack[a * NP3 * HD:(a + 1) * NP3 * HD, g, :, :],
                                 k_dram[hs, :, :, :].rearrange("h b d t -> (b d) h t")).then_inc(stack_in[g], 16)

            def load_ffn(b):
                sp.dma_start(w1_sb[:, :, :], w1[b, :, :].rearrange("(c p) h -> p c h", p=P)).then_inc(ffn_in, 16)
                sp.dma_start(w2_sb[:, :], w2[b, :, :]).then_inc(ffn_in, 16)

            def store_parts(b):
                q_rows = q_dram[:, 0:ROWS, :].rearrange("h (a e d) t -> h a e d t", a=NP3, e=NP3)
                sp.wait_ge(qk_split, 6 * b + 3)
                for a in range(NP3):
                    for e in range(NP3):
                        sp.dma_start(q_rows[:, a, e, :, :], parts[:, 0, a, :]).then_inc(scratch_w, 16)
                sp.wait_ge(qk_split, 6 * b + 6)
                for e in range(NP3):
                    sp.dma_start(k_dram[:, e, :, :], parts[:, 1, e, :]).then_inc(scratch_w, 16)

            def store_max(G, b, g):
                sp.wait_ge(max_split, 3 * G + 3)
                for a in range(NP3):
                    sp.dma_start(q_stack[ROWS + a:ROWS + a + 1, g, :, :].rearrange("o i (c t) -> o (i c) t", c=C),
                                 max_parts[:, a, :]).then_inc(max_in[g], 16)

            def store_u(b, g):
                sp.wait_ge(u_done, 4 * b + (g + 1))
                for j in range(GH):
                    sp.dma_start(u_dram[GH * g + j, :, :], u_sb[32 * j:32 * j + HD + 1, g, :]).then_inc(u_out[g], 16)

            def load_heads(b):
                for g in range(NG):
                    sp.wait_ge(u_out[g], 64 * b + 64)
                if not (isinstance(b, int) and b == 0):
                    sp.wait_ge(norm_done, b)
                sp.dma_start(den[:, :], u_dram[:, HD, :].rearrange("h (k t) -> h k t", k=HD)).then_inc(den_in, 16)
                sp.dma_start(heads[:, :], u_dram[:, 0:HD, :]).then_inc(heads_in, 16)

            def store_rden(b):
                sp.wait_ge(rden_done, b + 1)
                sp.dma_start(r_dram.rearrange("h (k t) -> (h k) t", k=HD), rden[:, :]).then_inc(rden_out, 16)

            def load_rden(b):
                sp.wait_ge(rden_out, 16 * b + 16)
                sp.dma_start(rden_all[:, :], r_dram.rearrange("h (o t) -> h o t", o=1).to_broadcast([H, HD, T])
                             ).then_inc(rden_in, 16)

            def store_y(b, index):
                sp.wait_ge(side_evac, index + 1)
                sp.dma_start(out[b, :, :].rearrange("(c p) d -> p c d", p=P), y[:, :, :]).then_inc(y_out, 16)

            def batch(b, kind):
                first, last = kind == "first", kind == "last"
                if not first:
                    sp.wait_ge(e_ready, 64 * b)
                load_stack(3, b)
                if not last:
                    if first:
                        sp.wait_ge(side_mm, turn(0, "prologue", "w12") + 1)
                    else:
                        sp.wait_ge(side_mm, b * len(MIDDLE) + (len(PROLOGUE) - 1 - len(MIDDLE) + MIDDLE.index("w12") + 1))
                    load_ffn(b + 1)
                if not first:
                    store_u(b - 1, 2)
                store_max(4 * b + 1, b, 1)
                if not last:
                    sp.wait_ge(stack_in[3], 64 * b + 64)
                    store_parts(b + 1)
                if not first:
                    store_u(b - 1, 3)
                store_max(4 * b + 2, b, 2)
                if not last:
                    sp.wait_ge(scratch_w, 192 * b + 384)
                    load_stack(0, b + 1)
                if not first:
                    load_heads(b - 1)
                if not last:
                    sp.wait_ge(e_ready, 64 * b + 32)
                    load_stack(1, b + 1)
                if not first:
                    sp.wait_ge(heads_in, 16 * b)
                    sp.wait_ge(den_in, 16 * b)
                store_u(b, 0)
                if not first:
                    store_rden(b - 1)
                store_max(4 * b + 3, b, 3)
                if not first:
                    load_rden(b - 1)
                if not last:
                    sp.wait_ge(e_ready, 64 * b + 48)
                    load_stack(2, b + 1)
                store_u(b, 1)
                if not last:
                    store_max(4 * b + 4, b + 1, 0)
                if not first:
                    store_y(b - 1, turn(b, kind, "out"))

            x_rows = x.rearrange("b (c p) d -> p (b c) d", p=P)
            x_sb = x_all[:, :].rearrange("p (n d) -> p n d", d=D)
            sp.dma_start(x_sb[:, 0:C, :], x_rows[:, 0:C, :]).then_inc(x0_in, 16)
            sp.dma_start(ident[:, :], identity).then_inc(const_in, 16)
            for dst, src in ((wq_sb, wq), (wk_sb, wk), (wv_sb, wv)):
                sp.dma_start(dst[:, :], src).then_inc(wqkv_in, 16)
            sp.wait_ge(const_in, 16)
            sp.dma_start(rope_sb[:, :, :], rope16.rearrange("(c p) n -> p c n", p=P)).then_inc(const_in, 16)
            sp.dma_start(mask_sb[:, :], headmask).then_inc(const_in, 16)
            sp.dma_start(wo_sb[:, :], wo).then_inc(const_in, 16)
            load_ffn(0)
            sp.dma_start(b1_rows[:, :], b1.rearrange("g (c p) -> (g c) p", p=P)).then_inc(bias_in, 16)
            sp.dma_start(b2_all[:, :], b2.rearrange("(o g) h -> o (g h)", o=1).to_broadcast([P, B * D])).then_inc(bias_in, 16)
            sp.dma_start(bo_all[:, :], bo.rearrange("(o d) -> o d", o=1).to_broadcast([P, D])).then_inc(bias_in, 16)
            sp.dma_start(x_sb[:, C:B * C, :], x_rows[:, C:B * C, :]).then_inc(x_in, 16)
            sp.wait_ge(filled, 3)
            sp.wait_ge(cleared, 2)
            sp.dma_start(q_dram[:, ROWS:QROWS, :], zero_rows[:, :].rearrange("h (r t) -> h r t", r=NP3)).then_inc(zeros_out, 16)
            store_parts(0)
            sp.wait_ge(zeros_out, 16)
            sp.wait_ge(scratch_w, 192)
            for g in range(3):
                load_stack(g, 0)
            store_max(0, 0, 0)
            batch(0, "first")
            with sp.Fori(1, B - 1) as b:
                batch(b, "middle")
            batch(B - 1, "last")
            store_u(B - 1, 2)
            store_u(B - 1, 3)
            load_heads(B - 1)
            store_rden(B - 1)
            load_rden(B - 1)
            store_y(B - 1, turn(B - 1, "last", "out") + 1)
            sp.wait_ge(y_out, 16 * B)


def kernel(L0_attn_x, L0_attn_Wq, L0_attn_Wk, L0_attn_Wv, L0_attn_Wo, L0_attn_bo, L0_ffn_W1, L0_ffn_b1, L0_ffn_W2,
           L0_ffn_b2):
    import concourse.bacc as bacc
    from concourse.bass_utils import run_bass_kernel_spmd

    half = HD // 2
    inv_freq = (1.0 / 10000.0 ** (np.arange(half, dtype=np.float32) / half)).astype(np.float32)
    angle = np.arange(T, dtype=np.float32)[:, None] * inv_freq[None, :]
    rope = np.concatenate([np.cos(angle), np.sin(angle)], axis=-1).astype(np.float32)
    arrays = {
        "x": L0_attn_x, "wq": L0_attn_Wq, "wk": L0_attn_Wk, "wv": L0_attn_Wv, "wo": L0_attn_Wo, "bo": L0_attn_bo,
        "w1": L0_ffn_W1, "b1": L0_ffn_b1, "w2": L0_ffn_W2, "b2": L0_ffn_b2,
        "rope16": np.tile(rope, (1, H)),
        "headmask": np.kron(np.eye(H, dtype=np.float32), np.ones((HD, HD), np.float32)),
        "identity": np.eye(P, dtype=np.float32),
    }
    arrays = {f"in_{n}": np.ascontiguousarray(a) for n, a in arrays.items()}
    nc = bacc.Bacc("TRN2", target_bir_lowering=False, num_devices=1)
    args = [nc.dram_tensor(n, a.shape, mybir.dt.from_np(a.dtype), kind="ExternalInput").ap() for n, a in arrays.items()]
    args.append(nc.dram_tensor("out_y", (B, T, D), F32, kind="ExternalOutput").ap())
    build(nc, *args)
    r = run_bass_kernel_spmd(nc, [arrays], core_ids=[0])
    return r.results[0]["out_y"]
```

```python
from contextlib import ExitStack

import numpy as np

import concourse.bass as bass
from concourse import mybir

F32 = mybir.dt.float32
BF16 = mybir.dt.bfloat16
ALU = mybir.AluOpType
ACT = mybir.ActivationFunctionType
AX_X = mybir.AxisListType.X

P = 128
B, T, D = 8, 512, 128
H, HD = 16, 8
C = T // P
GH = 4
NG = H // GH
FC = 512 // P
NP3 = 3
ROWS = NP3 * NP3 * HD
MAX_ROW = 96
EPS = 1e-5
ONES_PAIR = float(np.array([0x3F803F80], np.uint32).view(np.float32)[0])

TILES = H * C
BANK = [t % 3 for t in range(TILES - 1)] + [1]
REUSE = [next(d for d in range(1, 5) if BANK[t - d] == BANK[t]) for t in range(TILES)]

START = ["xnT", "q", "k", "v", "gram", "wo2", "b1T", "w2T", "w12", "ffn"]
PROLOGUE = ["max"]
MIDDLE = ["xnT", "max0", "q", "k", "max1", "v", "w2T", "w12", "ffn", "max2", "max3", "out"]
FIRST = [j for j in MIDDLE if j != "out"]
LAST = ["max0", "max1", "max2", "out"]


def turn(b, kind, job):
    if kind == "prologue":
        return PROLOGUE.index(job)
    if kind == "first":
        return len(PROLOGUE) + FIRST.index(job)
    jobs = {"middle": MIDDLE, "last": LAST}[kind]
    return b * len(MIDDLE) + (len(PROLOGUE) + len(FIRST) - len(MIDDLE) + jobs.index(job))


def build(nc, x, wq, wk, wv, wo, bo, w1, b1, w2, b2, rope16, headmask, identity, out):
    with ExitStack() as ctx:
        def sb(name, shape, dt):
            return ctx.enter_context(nc.sbuf_tensor(name, shape, dt))

        def sem(name):
            return ctx.enter_context(nc.semaphore(name))

        ident = sb("ident", [P, P], F32)
        ident_b = sb("ident_b", [P, P], BF16)
        ones = sb("ones", [P, P], F32)
        rope_sb = sb("rope_sb", [P, C, P], F32)
        mask_sb = sb("mask_sb", [P, P], F32)
        gram = sb("gram", [P, P], F32)
        wq_sb = sb("wq_sb", [P, D], F32)
        wk_sb = sb("wk_sb", [P, D], F32)
        wv_sb = sb("wv_sb", [P, D], F32)
        wo_sb = sb("wo_sb", [P, D], F32)
        wo2 = sb("wo2", [P, D], F32)
        w1_sb = sb("w1_sb", [P, FC, D], F32)
        w2_sb = sb("w2_sb", [P, FC * P], F32)
        w2T = sb("w2T", [P, FC, D], F32)
        w12 = sb("w12", [P, D], F32)
        b1_rows = sb("b1_rows", [B * FC, P], F32)
        b1T = sb("b1T", [P, B * FC], F32)
        b1_now = sb("b1_now", [P, FC], F32)
        b1w2 = sb("b1w2", [P, FC, D], F32)
        b2_all = sb("b2_all", [P, B * D], F32)
        bo_all = sb("bo_all", [P, D], F32)
        bias = sb("bias", [P, D], F32)
        x_all = sb("x_all", [P, B * C * D], F32)
        stats = sb("stats", [P, B * C, 6], F32)
        mv = sb("mv", [P, B * C, 2], F32)
        rstd = sb("rstd", [P, B * C], F32)
        half = sb("half", [P, B * C], F32)
        xn = sb("xn", [P, C, D], F32)
        xnT = sb("xnT", [P, T], F32)
        qk_f = sb("qk_f", [P, 2, T], F32)
        qk_r = sb("qk_r", [P, 2, T], F32)
        parts = sb("parts", [P, 2, NP3, T], BF16)
        q_stack = sb("q_stack", [P, NG, GH, T], BF16)
        k_stack = sb("k_stack", [P, NG, GH, T], BF16)
        v_stage = sb("v_stage", [P, C, H, HD], F32)
        v_ones = sb("v_ones", [P, C, H, 32], F32)
        negmax = sb("negmax", [P, 2, GH * C], F32)
        zero16 = sb("zero16", [P, GH * C], F32)
        max_r = sb("max_r", [P, GH * C], F32)
        max_parts = sb("max_parts", [P, 2, P // (GH * C), GH * C], BF16)
        max_rows = sb("max_rows", [NP3 * GH * C, P], BF16)
        probs = sb("probs", [P, 2, GH, C, T], F32)
        u_sb = sb("u_sb", [P, NG, T], F32)
        heads = sb("heads", [P, T], F32)
        den = sb("den", [P, T // HD], F32)
        rden = sb("rden", [P, T // HD], F32)
        rden_all = sb("rden_all", [P, T], F32)
        headsn = sb("headsn", [P, T], F32)
        y_base = sb("y_base", [P, B * C * D], F32)
        y = sb("y", [P, C, D], F32)

        q_dram = nc.dram_tensor("q_scratch", [H, HD, NP3, NP3, T], BF16).ap()
        k_dram = nc.dram_tensor("k_scratch", [H, HD, NP3, NP3, T], BF16).ap()
        u_dram = nc.dram_tensor("u_scratch", [H, HD + 1, T], F32).ap()
        r_dram = nc.dram_tensor("r_scratch", [H, T], F32).ap()

        ps_m = ctx.enter_context(nc.psum_tensor("ps_m", [P, 3, T], F32))
        ps_e = ctx.enter_context(nc.psum_tensor("ps_e", [P, 3, T], F32))
        ps_u = ctx.enter_context(nc.psum_tensor("ps_u", [P, T], F32))
        ps_side = ctx.enter_context(nc.psum_tensor("ps_side", [P, T], F32))

        x0_in, x_in, wqkv_in, ffn_in, const_in, bias_in = map(
            sem, ["x0_in", "x_in", "wqkv_in", "ffn_in", "const_in", "bias_in"])
        filled, cleared = sem("filled"), sem("cleared")
        ln_stat, ln_rstd, xn_ready = map(sem, ["ln_stat", "ln_rstd", "xn_ready"])
        ident_ready = sem("ident_ready")
        start_mm, start_act, start_dve = sem("start_mm"), sem("start_act"), sem("start_dve")
        side_mm, side_evac = sem("side_mm"), sem("side_evac")
        qk_split, scratch_w = sem("qk_split"), sem("scratch_w")
        k_split = sem("k_split")
        stack_in = [sem(f"stack_in{g}") for g in range(NG)]
        v_copied = sem("v_copied")
        b1_copied, b1w2_done = sem("b1_copied"), sem("b1w2_done")
        bias_done, base_done = sem("bias_done"), sem("base_done")
        m_ready, m_done, max_split = map(sem, ["m_ready", "m_done", "max_split"])
        max_in = [sem(f"max_in{g}") for g in range(NG)]
        e_ready, e_done, pv_done, u_done = map(sem, ["e_ready", "e_done", "pv_done", "u_done"])
        u_out = [sem(f"u_out{g}") for g in range(NG)]
        heads_in, den_in, rden_done, rden_out, rden_in, norm_done = map(
            sem, ["heads_in", "den_in", "rden_done", "rden_out", "rden_in", "norm_done"])
        y_out = sem("y_out")

        block = ctx.enter_context(nc.Block())

        def last_done(b, kind, job):
            if kind == "first":
                return start_mm, START.index(job) + 1
            return side_mm, b * len(MIDDLE) + (len(PROLOGUE) + len(FIRST) - 2 * len(MIDDLE) + MIDDLE.index(job) + 1)

        start_bank = {"xnT": ps_side[:, :], "q": ps_m[:, 0, :], "k": ps_m[:, 1, :], "v": ps_m[:, 2, :],
                      "gram": ps_e[:, 0, :], "wo2": ps_e[:, 1, :], "b1T": ps_e[:, 2, :], "w2T": ps_u[:, :],
                      "w12": ps_e[:, 0, :], "ffn": ps_e[:, 1, :]}

        def started(job):
            return START.index(job) + 1

        @block.tensor
        def _(pe):
            def side(index):
                if not (isinstance(index, int) and index == 0):
                    pe.wait_ge(side_evac, index)

            def transpose4(bank, done, src):
                for c in range(4):
                    last = nc.tensor.transpose(bank[:, c * P:(c + 1) * P], src(c), ident[:, :])
                last.then_inc(done, 1)

            def job_xnT(b, bank, done):
                pe.wait_ge(xn_ready, 4 * b + 4)
                transpose4(bank, done, lambda c: xn[:, c, :])

            def job_project(bank, done, w):
                nc.tensor.matmul(bank, w[:, :], xnT[:, :], start=True, stop=True).then_inc(done, 1)

            def job_tokens(bank, done, lhsT, w):
                for c in range(C):
                    last = nc.tensor.matmul(bank[:, c * D:(c + 1) * D], lhsT[:, c * P:(c + 1) * P], w[:, :],
                                            start=True, stop=True)
                last.then_inc(done, 1)

            def job_w2T(b, bank, done):
                pe.wait_ge(ffn_in, 32 * b + 32)
                transpose4(bank, done, lambda c: w2_sb[:, c * P:(c + 1) * P])

            def job_w12(b, bank, done):
                for c in range(FC):
                    nc.tensor.matmul(bank[:, 0:D], w1_sb[:, c, :], w2T[:, c, :], start=(c == 0), stop=(c == FC - 1))
                pe.wait_ge(b1w2_done, 3 * b + 3)
                nc.tensor.matmul(bank[:, D:2 * D], ones[:, :], b1w2[:, 0, :], start=True, stop=True).then_inc(done, 1)

            def job_max(G, parity, index):
                side(index)
                pe.wait_ge(max_split, 4 * G + 4)
                nc.tensor.transpose(ps_side[:, 0:P // 2].bitcast(BF16),
                                    max_parts[:, parity, :, :].rearrange("p a n -> p (a n)"), ident_b[:, :]
                                    ).then_inc(side_mm, 1)

            def free_bank(done, b, tile):
                count = TILES * b + (tile - REUSE[tile] + 1)
                if not (isinstance(count, int) and count < 1):
                    pe.wait_ge(done, count)

            def m_tile(b, g, i, c):
                tile = GH * C * g + C * i + c
                free_bank(m_done, b, tile)
                nc.tensor.matmul(ps_m[:, BANK[tile], :], q_stack[0:MAX_ROW, g, i, c * P:(c + 1) * P],
                                 k_stack[0:MAX_ROW, g, i, :], start=True, stop=True).then_inc(m_ready, 1)

            def e_tile(b, g, i, c):
                tile = GH * C * g + C * i + c
                free_bank(e_done, b, tile)
                nc.tensor.matmul(ps_e[:, BANK[tile], :], k_stack[:, g, i, c * P:(c + 1) * P], q_stack[:, g, i, :],
                                 start=True, stop=True).then_inc(e_ready, 1)

            def pv_chunk(G, g, c):
                if c == 0:
                    pe.wait_ge(e_done, 16 * G + 16)
                    if not (isinstance(G, int) and G == 0):
                        pe.wait_ge(u_done, G)
                for j in range(GH):
                    last = nc.tensor.matmul(ps_u[32 * j:32 * j + 32, :], v_ones[:, c, GH * g + j, :],
                                            probs[:, g % 2, j, c, :], start=(c == 0), stop=(c == C - 1))
                last.then_inc(pv_done, 1)

            def step(b, s, kind, jobs):
                G = 4 * b + s
                do_m = kind != "last" or s < 2
                do_pv = not (kind == "first" and s == 0)
                g_m = (s + 2) % NG
                b_m = b if s < 2 else b + 1
                for i in range(GH):
                    if i == 0:
                        pe.wait_ge(max_in[s], 16 * b + 16)
                        if do_m:
                            pe.wait_ge(stack_in[g_m], 32 * b_m + 32)
                    for c in range(2):
                        e_tile(b, s, i, c)
                        if do_m:
                            m_tile(b_m, g_m, i, c)
                    if (i, 0) in jobs:
                        jobs[i, 0]()
                    if do_pv:
                        if s == 1:
                            pe.wait_ge(v_copied, 4 * b + (i + 1))
                        pv_chunk(G - 1, (s - 1) % NG, i)
                    for c in range(2, 4):
                        e_tile(b, s, i, c)
                        if do_m:
                            m_tile(b_m, g_m, i, c)
                    if (i, 1) in jobs:
                        jobs[i, 1]()

            def batch(b, kind):
                def on_side(name, job, *args):
                    def run():
                        side(turn(b, kind, name))
                        job(*args)
                    return run

                bank, done = ps_side[:, :], side_mm
                prepare0 = {} if kind == "last" else {
                    (0, 1): on_side("xnT", job_xnT, b + 1, bank, done),
                    (1, 1): on_side("q", job_project, bank, done, wq_sb),
                    (2, 0): on_side("k", job_project, bank, done, wk_sb)}
                prepare1 = {} if kind == "last" else {
                    (1, 0): on_side("v", job_tokens, bank, done, xnT, wv_sb),
                    (1, 1): on_side("w2T", job_w2T, b + 1, bank, done),
                    (2, 1): on_side("w12", job_w12, b + 1, bank, done),
                    (3, 1): on_side("ffn", job_tokens, bank, done, xnT, w12)}
                step(b, 0, kind, prepare0 | {(1, 0): lambda: job_max(4 * b + 1, 1, turn(b, kind, "max0"))})
                step(b, 1, kind, prepare1 | {(0, 1): lambda: job_max(4 * b + 2, 0, turn(b, kind, "max1"))})
                step(b, 2, kind, {(0, 1): lambda: job_max(4 * b + 3, 1, turn(b, kind, "max2"))})
                jobs = {}
                if kind != "last":
                    jobs[0, 1] = lambda: job_max(4 * b + 4, 0, turn(b, kind, "max3"))
                if kind != "first":
                    def output():
                        pe.wait_ge(norm_done, b)
                        job_tokens(bank, done, headsn, wo2)
                    jobs[2, 0] = on_side("out", output)
                step(b, 3, kind, jobs)

            at, done = start_bank, start_mm
            pe.wait_ge(const_in, 16)
            job_xnT(0, at["xnT"], done)
            pe.wait_ge(wqkv_in, 48)
            pe.wait_ge(start_act, 1)
            job_project(at["q"], done, wq_sb)
            job_project(at["k"], done, wk_sb)
            job_tokens(at["v"], done, xnT, wv_sb)
            pe.wait_ge(const_in, 64)
            for c in range(C):
                last = nc.tensor.matmul(at["gram"][:, 0:P], rope_sb[:, c, :], rope_sb[:, c, :],
                                        start=(c == 0), stop=(c == C - 1))
            last.then_inc(done, 1)
            pe.wait_ge(start_dve, 2)
            nc.tensor.matmul(at["wo2"][:, 0:D], gram[:, :], wo_sb[:, :], start=True, stop=True).then_inc(done, 1)
            pe.wait_ge(bias_in, 48)
            nc.tensor.transpose(at["b1T"][:, 0:B * FC], b1_rows[:, :], ident[0:B * FC, 0:B * FC]).then_inc(done, 1)
            job_w2T(0, at["w2T"], done)
            pe.wait_ge(start_act, 3)
            for G in range(2):
                pe.wait_ge(stack_in[G], 32)
                for i in range(GH):
                    for c in range(C):
                        m_tile(0, G, i, c)
                    if G == 1 and i == 0:
                        pe.wait_ge(start_act, 6)
                        job_w12(0, at["w12"], done)
                    if G == 1 and i == 1:
                        job_max(0, 0, turn(0, "prologue", "max"))
                    if G == 1 and i == 2:
                        pe.wait_ge(start_dve, 3)
                        job_tokens(at["ffn"], done, xnT, w12)
            pe.wait_ge(start_dve, 4)
            batch(0, "first")
            with pe.Fori(1, B - 1) as b:
                batch(b, "middle")
            batch(B - 1, "last")
            for c in range(C):
                pv_chunk(4 * B - 1, NG - 1, c)
            side(turn(B - 1, "last", "out") + 1)
            pe.wait_ge(norm_done, B)
            job_tokens(ps_side[:, :], side_mm, headsn, wo2)

        @block.scalar
        def _(act):
            def evac(index, pairs):
                act.wait_ge(side_mm, index + 1)
                for dst, src in pairs:
                    last = nc.scalar.activation(dst, src, ACT.Copy)
                last.then_inc(side_evac, 1)

            def evac_qk(b, index, o):
                if True:
                    act.wait_ge(scratch_w, 96 * b)
                evac(index, [(qk_f[:, o, :], ps_side[:, :]), (parts[:, o, 0, :], ps_side[:, :])])

            def evac_v(b, index):
                evac(index, [(v_stage[:, :, :, :].rearrange("p c h d -> p (c h d)"), ps_side[:, :])])

            def copy_v(c):
                nc.scalar.activation(v_ones[:, c, :, 0:HD], v_stage[:, c, :, :], ACT.Copy).then_inc(v_copied, 1)

            def evac_max(b, s, index):
                if not (isinstance(b, int) and b == 0 and s == 0):
                    before = b if s > 0 else b - 1
                    act.wait_ge(max_in[(s - 1) % NG], 16 * before + 16)
                evac(index, [(max_rows[:, :], ps_side[0:NP3 * GH * C, 0:P // 2].bitcast(BF16))])

            def evac_u(b, G, g):
                act.wait_ge(pv_done, 4 * G + 4)
                if not (isinstance(b, int) and b == 0):
                    act.wait_ge(u_out[g], 64 * b)
                nc.scalar.activation(u_sb[:, g, :], ps_u[:, :], ACT.Copy).then_inc(u_done, 1)

            def step(b, s, kind, jobs):
                G = 4 * b + s
                for i in range(GH):
                    for c in range(C):
                        if c == 2:
                            if (i, 0) in jobs:
                                jobs[i, 0]()
                            if i == GH - 1 and not (kind == "first" and s == 0):
                                evac_u(b if s > 0 else b - 1, G - 1, (s - 1) % NG)
                        if c == 3 and s == 0 and kind != "first":
                            act.wait_ge(pv_done, 16 * b + (i - 3))
                            copy_v(i)
                        act.wait_ge(e_ready, 16 * G + (4 * i + c + 1))
                        nc.scalar.activation(probs[:, s % 2, i, c, :], ps_e[:, BANK[16 * s + 4 * i + c], :], ACT.Exp,
                                             scale=float(HD) ** -0.5).then_inc(e_done, 1)
                    if (i, 1) in jobs:
                        jobs[i, 1]()

            def batch(b, kind):
                t = lambda job: turn(b, kind, job)
                flat = xnT[:, :]
                step(b, 0, kind, {(1, 0): lambda: evac_max(b, 1, t("max0"))} | ({} if kind == "last" else {
                    (0, 1): lambda: evac(t("xnT"), [(flat, ps_side[:, :])]),
                    (1, 1): lambda: evac_qk(b + 1, t("q"), 0),
                    (2, 0): lambda: evac_qk(b + 1, t("k"), 1)}))
                step(b, 1, kind, {(0, 1): lambda: evac_max(b, 2, t("max1"))} | ({} if kind == "last" else {
                    (1, 0): lambda: evac_v(b + 1, t("v")),
                    (1, 1): lambda: evac(t("w2T"), [(w2T[:, :, :].rearrange("p c h -> p (c h)"), ps_side[:, :])]),
                    }))
                step(b, 2, kind, {(0, 1): lambda: evac_max(b, 3, t("max2"))})
                step(b, 3, kind, {} if kind == "last" else {(0, 1): lambda: evac_max(b + 1, 0, t("max3"))})

            def start_evac(job, pairs):
                act.wait_ge(start_mm, started(job))
                for dst, src in pairs:
                    last = nc.scalar.activation(dst, src, ACT.Copy)
                last.then_inc(start_act, 1)

            at = start_bank
            start_evac("xnT", [(xnT[:, :], at["xnT"])])
            start_evac("q", [(parts[:, 0, 0, :], at["q"]), (qk_f[:, 0, :], at["q"])])
            start_evac("v", [(v_stage[:, :, :, :].rearrange("p c h d -> p (c h d)"), at["v"])])
            act.wait_ge(filled, 1)
            act.wait_ge(start_act, 3)
            for c in range(C):
                copy_v(c)
            start_evac("wo2", [(wo2[:, :], at["wo2"][:, 0:D])])
            start_evac("b1T", [(b1T[:, :], at["b1T"][:, 0:B * FC])])
            start_evac("w2T", [(w2T[:, :, :].rearrange("p c h -> p (c h)"), at["w2T"])])
            evac_max(0, 0, turn(0, "prologue", "max"))
            batch(0, "first")
            with act.Fori(1, B - 1) as b:
                batch(b, "middle")
            batch(B - 1, "last")
            evac_u(B - 1, 4 * B - 1, NG - 1)

        @block.vector
        def _(dve):
            def stat(c0, c1):
                for c in range(c0, c1):
                    last = nc.vector.bn_stats(stats[:, c, :], x_all[:, c * D:(c + 1) * D])
                last.then_inc(ln_stat, 1)

            def aggregate(c0, c1, count):
                dve.wait_ge(ln_stat, count)
                for c in range(c0, c1):
                    last = nc.vector.bn_aggr(mv[:, c, :], stats[:, c, :])
                last.then_inc(ln_stat, 1)

            def normalise(b, kind):
                dve.wait_ge(*last_done(b, kind, "xnT"))
                for c in range(C):
                    nc.vector.tensor_scalar(xn[:, c, :], x_all[:, bass.ds(b * (C * D) + (C + c) * D, D)],
                                            mv[:, bass.ds(b * C + (C + c), 1), 0], rstd[:, bass.ds(b * C + (C + c), 1)],
                                            ALU.subtract, ALU.mult).then_inc(xn_ready, 1)

            def reduce_tile(b, g, i, c):
                tile = GH * C * g + C * i + c
                dve.wait_ge(m_ready, TILES * b + (tile + 1))
                nc.vector.tensor_reduce(negmax[:, g % 2, C * i + c:C * i + c + 1], ps_m[:, BANK[tile], :],
                                        AX_X, ALU.max, negate=True).then_inc(m_done, 1)

            def reciprocals(b):
                dve.wait_ge(den_in, 16 * b + 16)
                if not (isinstance(b, int) and b == 0):
                    dve.wait_ge(rden_out, 16 * b)
                nc.vector.reciprocal(rden[:, :], den[:, :]).then_inc(rden_done, 1)

            def finish(b, index):
                dve.wait_ge(side_mm, index + 1)
                if not (isinstance(b, int) and b == 0):
                    dve.wait_ge(y_out, 16 * b)
                nc.vector.tensor_tensor(y[:, :, :].rearrange("p c d -> p (c d)"), ps_side[:, :],
                                        y_base[:, bass.ds(b * (C * D), C * D)], ALU.add).then_inc(side_evac, 1)

            def evac_w12(b, bank, done):
                nc.vector.tensor_copy(w12[:, :], bank[:, 0:D])
                nc.vector.tensor_tensor(bias[:, :], bank[:, D:2 * D], b2_all[:, bass.ds(b * D, D)],
                                        ALU.add).then_inc(done, 1)

            def evac_ffn(b, bank, done, count):
                rows = y_base[:, bass.ds(b * (C * D), C * D)]
                nc.vector.tensor_tensor(rows, bank, x_all[:, bass.ds(b * (C * D), C * D)], ALU.add).then_inc(done, 1)
                dve.wait_ge(done, count)
                rows4 = rows.rearrange("p (c d) -> p c d", c=C)
                nc.vector.tensor_tensor(rows4, rows4, bias[:, :].rearrange("p (o d) -> p o d", o=1).to_broadcast([P, C, D]),
                                        ALU.add).then_inc(base_done, 1)

            def step(b, s, kind, jobs):
                do_m = kind != "last" or s < 2
                for i in range(GH):
                    for c in range(C):
                        if do_m:
                            reduce_tile(b if s < 2 else b + 1, (s + 2) % NG, i, c)
                        if c % 2 and (i, c // 2) in jobs:
                            jobs[i, c // 2]()

            def batch(b, kind):
                t = lambda job: turn(b, kind, job)

                def side_w12():
                    dve.wait_ge(side_mm, t("w12") + 1)
                    evac_w12(b + 1, ps_side[:, :], side_evac)

                def side_ffn():
                    dve.wait_ge(side_mm, t("ffn") + 1)
                    evac_ffn(b + 1, ps_side[:, :], side_evac, t("ffn") + 1)

                if kind != "last":
                    normalise(b, kind)
                step(b, 0, kind, {})
                step(b, 1, kind, ({} if kind == "first" else {(3, 0): lambda: reciprocals(b - 1)}) |
                     ({} if kind == "last" else {(2, 1): side_w12, (3, 1): side_ffn}))
                step(b, 2, kind, {})
                step(b, 3, kind, {} if kind == "first" else {(2, 0): lambda: finish(b - 1, t("out"))})

            nc.vector.memset(half[:, :], -0.5).then_inc(cleared, 1)
            nc.vector.memset(zero16[:, :], 0.0).then_inc(cleared, 1)
            nc.vector.memset(max_parts[:, :, :, :], 0.0).then_inc(cleared, 1)
            nc.vector.memset(ones[:, :], 1.0).then_inc(cleared, 1)
            dve.wait_ge(x0_in, 16)
            stat(0, C)
            aggregate(0, C, 1)
            dve.wait_ge(ln_rstd, 2)
            for c in range(C):
                nc.vector.tensor_scalar(xn[:, c, :], x_all[:, c * D:(c + 1) * D], mv[:, c:c + 1, 0], rstd[:, c:c + 1],
                                        ALU.subtract, ALU.mult).then_inc(xn_ready, 1)
            nc.vector.memset(q_stack[64:P, :, :, :].rearrange("p g i t -> p (g i t)").bitcast(F32), 0.0).then_inc(cleared, 1)
            at = start_bank
            dve.wait_ge(start_mm, started("k"))
            nc.vector.tensor_copy(parts[:, 1, 0, :], at["k"]).then_inc(k_split, 1)
            dve.wait_ge(k_split, 1)
            nc.vector.tensor_tensor(qk_r[:, 1, :], at["k"], parts[:, 1, 0, :], ALU.subtract).then_inc(k_split, 1)
            dve.wait_ge(k_split, 2)
            nc.vector.tensor_copy(parts[:, 1, 1, :], qk_r[:, 1, :]).then_inc(k_split, 1)
            dve.wait_ge(k_split, 3)
            nc.vector.tensor_tensor(parts[:, 1, 2, :], qk_r[:, 1, :], parts[:, 1, 1, :], ALU.subtract).then_inc(start_dve, 1)
            dve.wait_ge(start_mm, started("gram"))
            dve.wait_ge(const_in, 64)
            nc.vector.tensor_tensor(gram[:, :], at["gram"][:, 0:P], mask_sb[:, :], ALU.mult).then_inc(start_dve, 1)
            nc.vector.tensor_copy(ident_b[:, :], ident[:, :]).then_inc(ident_ready, 1)
            dve.wait_ge(x_in, 16)
            stat(C, B * C)
            aggregate(C, B * C, 3)
            dve.wait_ge(bias_in, 48)
            nc.vector.tensor_tensor(b2_all[:, :].rearrange("p (g d) -> p g d", g=B), b2_all[:, :].rearrange("p (g d) -> p g d", g=B),
                                    bo_all[:, :].rearrange("p (o d) -> p o d", o=1).to_broadcast([P, B, D]),
                                    ALU.add).then_inc(bias_done, 1)
            dve.wait_ge(bias_done, 1)
            for G in range(2):
                for i in range(GH):
                    for c in range(C):
                        reduce_tile(0, G, i, c)
                    if G == 1 and i == 1:
                        dve.wait_ge(start_mm, started("w12"))
                        evac_w12(0, at["w12"], start_dve)
                    if G == 1 and i == 3:
                        dve.wait_ge(start_mm, started("ffn"))
                        evac_ffn(0, at["ffn"], start_dve, 4)
            dve.wait_ge(ln_rstd, 4)
            batch(0, "first")
            with dve.Fori(1, B - 1) as b:
                batch(b, "middle")
            batch(B - 1, "last")
            reciprocals(B - 1)
            finish(B - 1, turn(B - 1, "last", "out") + 1)

        @block.gpsimd
        def _(pool):
            def split_qk(count, o):
                nc.gpsimd.tensor_tensor(parts[:, o, 1, :], qk_f[:, o, :], parts[:, o, 0, :],
                                        ALU.subtract).then_inc(qk_split, 1)
                nc.gpsimd.tensor_tensor(qk_r[:, o, :], qk_f[:, o, :], parts[:, o, 0, :],
                                        ALU.subtract).then_inc(qk_split, 1)
                pool.wait_ge(qk_split, count + 2)
                nc.gpsimd.tensor_tensor(parts[:, o, 2, :], qk_r[:, o, :], parts[:, o, 1, :],
                                        ALU.subtract).then_inc(qk_split, 1)

            def split_max(G, parity):
                pool.wait_ge(m_done, 16 * G + 16)
                nc.gpsimd.tensor_tensor(max_parts[:, parity, 0, :], negmax[:, parity, :], zero16[:, :],
                                        ALU.add).then_inc(max_split, 1)
                pool.wait_ge(max_split, 4 * G + 1)
                nc.gpsimd.tensor_tensor(max_parts[:, parity, 1, :], negmax[:, parity, :], max_parts[:, parity, 0, :],
                                        ALU.subtract).then_inc(max_split, 1)
                nc.gpsimd.tensor_tensor(max_r[:, :], negmax[:, parity, :], max_parts[:, parity, 0, :],
                                        ALU.subtract).then_inc(max_split, 1)
                pool.wait_ge(max_split, 4 * G + 3)
                nc.gpsimd.tensor_tensor(max_parts[:, parity, 2, :], max_r[:, :], max_parts[:, parity, 1, :],
                                        ALU.subtract).then_inc(max_split, 1)

            def multiply_b1(b):
                pool.wait_ge(b1_copied, b + 1)
                nc.gpsimd.tensor_tensor(b1w2[:, :, :], w2T[:, :, :],
                                        b1_now[:, :].rearrange("p (c o) -> p c o", o=1).to_broadcast([P, FC, D]),
                                        ALU.mult).then_inc(b1w2_done, 1)
                pool.wait_ge(b1w2_done, 3 * b + 1)
                nc.gpsimd.tensor_tensor(b1w2[:, 0:2, :], b1w2[:, 0:2, :], b1w2[:, 2:4, :], ALU.add).then_inc(b1w2_done, 1)
                pool.wait_ge(b1w2_done, 3 * b + 2)
                nc.gpsimd.tensor_tensor(b1w2[:, 0, :], b1w2[:, 0, :], b1w2[:, 1, :], ALU.add).then_inc(b1w2_done, 1)

            def copy_b1(b):
                nc.gpsimd.tensor_copy(b1_now[:, :], b1T[:, bass.ds(b * FC, FC)]).then_inc(b1_copied, 1)

            def norm(b):
                pool.wait_ge(heads_in, 16 * b + 16)
                pool.wait_ge(rden_in, 16 * b + 16)
                nc.gpsimd.tensor_tensor(headsn[:, :], heads[:, :], rden_all[:, :], ALU.mult).then_inc(norm_done, 1)

            def batch(b, kind):
                t = lambda job: turn(b, kind, job)
                split_max(4 * b + 1, 1)
                if kind != "last":
                    pool.wait_ge(side_evac, t("q") + 1)
                    split_qk(6 * b + 3, 0)
                    pool.wait_ge(side_evac, t("k") + 1)
                    split_qk(6 * b + 6, 1)
                    copy_b1(b + 1)
                split_max(4 * b + 2, 0)
                if kind != "last":
                    pool.wait_ge(side_evac, t("w2T") + 1)
                    multiply_b1(b + 1)
                split_max(4 * b + 3, 1)
                if kind != "last":
                    split_max(4 * b + 4, 0)
                if kind != "first":
                    norm(b - 1)

            def inverse_std(c0, c1, stat_count, rstd_count):
                pool.wait_ge(ln_stat, stat_count)
                nc.gpsimd.tensor_scalar(rstd[:, c0:c1], mv[:, c0:c1, 1], 1.0, EPS, ALU.mult, ALU.add).then_inc(ln_rstd, 1)
                pool.wait_ge(ln_rstd, rstd_count)
                nc.gpsimd.tensor_tensor(rstd[:, c0:c1], rstd[:, c0:c1], half[:, c0:c1], ALU.pow).then_inc(ln_rstd, 1)

            nc.gpsimd.memset(v_ones[:, :, :, :], 1.0).then_inc(filled, 1)
            pool.wait_ge(filled, 1)
            pool.wait_ge(cleared, 3)
            inverse_std(0, C, 2, 1)
            pool.wait_ge(ln_rstd, 2)
            nc.gpsimd.memset(k_stack[64:P, :, :, :].rearrange("p g i t -> p (g i t)").bitcast(F32),
                             ONES_PAIR).then_inc(filled, 1)
            pool.wait_ge(filled, 2)
            pool.wait_ge(start_act, 2)
            split_qk(0, 0)
            pool.wait_ge(start_act, 5)
            copy_b1(0)
            inverse_std(C, B * C, 4, 3)
            pool.wait_ge(start_act, 6)
            multiply_b1(0)
            split_max(0, 0)
            batch(0, "first")
            with pool.Fori(1, B - 1) as b:
                batch(b, "middle")
            batch(B - 1, "last")
            pool.wait_ge(side_mm, turn(B - 1, "last", "out") + 1)
            norm(B - 1)

        @block.sync
        def _(sp):
            def load_stack(g, b):
                hs = slice(GH * g, GH * g + GH)
                for stack, scratch in ((q_stack, q_dram), (k_stack, k_dram)):
                    sp.dma_start(stack[0:ROWS, g, :, :], scratch[hs].rearrange("h d a e t -> (d a e) h t")
                                 ).then_inc(stack_in[g], 16)

            def load_ffn(b):
                sp.dma_start(w1_sb[:, :, :], w1[b, :, :].rearrange("(c p) h -> p c h", p=P)).then_inc(ffn_in, 16)
                sp.dma_start(w2_sb[:, :], w2[b, :, :]).then_inc(ffn_in, 16)

            def store_q():
                for e in range(NP3):
                    sp.dma_start(q_dram[:, :, :, e, :].rearrange("h d a t -> (h d) a t"), parts[:, 0, :, :]).then_inc(scratch_w, 16)

            def store_k():
                for a in range(NP3):
                    sp.dma_start(k_dram[:, :, a, :, :].rearrange("h d e t -> (h d) e t"), parts[:, 1, :, :]).then_inc(scratch_w, 16)

            def store_max(index, g):
                sp.wait_ge(side_evac, index + 1)
                sp.dma_start(q_stack[MAX_ROW:MAX_ROW + NP3, g, :, :].rearrange("a i (c t) -> a (i c) t", c=C),
                             max_rows[:, :]).then_inc(max_in[g], 16)

            def store_u(b, g):
                sp.wait_ge(u_done, 4 * b + (g + 1))
                for j in range(GH):
                    sp.dma_start(u_dram[GH * g + j, :, :], u_sb[32 * j:32 * j + HD + 1, g, :]).then_inc(u_out[g], 16)

            def load_heads(b):
                for g in range(NG):
                    sp.wait_ge(u_out[g], 64 * b + 64)
                if not (isinstance(b, int) and b == 0):
                    sp.wait_ge(norm_done, b)
                sp.dma_start(den[:, :], u_dram[:, HD, :].rearrange("h (k t) -> h k t", k=HD)).then_inc(den_in, 16)
                sp.dma_start(heads[:, :], u_dram[:, 0:HD, :]).then_inc(heads_in, 16)

            def store_rden(b):
                sp.wait_ge(rden_done, b + 1)
                sp.dma_start(r_dram.rearrange("h (k t) -> (h k) t", k=HD), rden[:, :]).then_inc(rden_out, 16)

            def load_rden(b):
                sp.wait_ge(rden_out, 16 * b + 16)
                sp.dma_start(rden_all[:, :], r_dram.rearrange("h (o t) -> h o t", o=1).to_broadcast([H, HD, T])
                             ).then_inc(rden_in, 16)

            def store_y(b, index):
                sp.wait_ge(side_evac, index + 1)
                sp.dma_start(out[b, :, :].rearrange("(c p) d -> p c d", p=P), y[:, :, :]).then_inc(y_out, 16)

            def batch(b, kind):
                first, last = kind == "first", kind == "last"
                t = lambda job: turn(b, kind, job)
                if not first:
                    sp.wait_ge(e_ready, 64 * b)
                load_stack(3, b)
                if not last:
                    sp.wait_ge(*last_done(b, kind, "w12"))
                    load_ffn(b + 1)
                if not first:
                    store_u(b - 1, 2)
                store_max(t("max0"), 1)
                if not last:
                    sp.wait_ge(stack_in[3], 32 * b + 32)
                    sp.wait_ge(qk_split, 6 * b + 6)
                    store_q()
                    sp.wait_ge(qk_split, 6 * b + 9)
                    store_k()
                if not first:
                    store_u(b - 1, 3)
                store_max(t("max1"), 2)
                if not last:
                    sp.wait_ge(scratch_w, 96 * b + 192)
                    load_stack(0, b + 1)
                if not first:
                    load_heads(b - 1)
                if not last:
                    sp.wait_ge(e_ready, 64 * b + 32)
                    load_stack(1, b + 1)
                if not first:
                    sp.wait_ge(heads_in, 16 * b)
                    sp.wait_ge(den_in, 16 * b)
                store_u(b, 0)
                if not first:
                    store_rden(b - 1)
                store_max(t("max2"), 3)
                if not first:
                    load_rden(b - 1)
                if not last:
                    sp.wait_ge(e_ready, 64 * b + 48)
                    load_stack(2, b + 1)
                store_u(b, 1)
                if not last:
                    store_max(t("max3"), 0)
                if not first:
                    store_y(b - 1, turn(b, kind, "out"))

            x_rows = x.rearrange("b (c p) d -> p (b c) d", p=P)
            x_sb = x_all[:, :].rearrange("p (n d) -> p n d", d=D)
            sp.dma_start(x_sb[:, 0:C, :], x_rows[:, 0:C, :]).then_inc(x0_in, 16)
            sp.dma_start(ident[:, :], identity).then_inc(const_in, 16)
            for dst, src in ((wq_sb, wq), (wk_sb, wk), (wv_sb, wv)):
                sp.dma_start(dst[:, :], src).then_inc(wqkv_in, 16)
            sp.wait_ge(const_in, 16)
            sp.dma_start(rope_sb[:, :, :], rope16.rearrange("(c p) n -> p c n", p=P)).then_inc(const_in, 16)
            sp.dma_start(mask_sb[:, :], headmask).then_inc(const_in, 16)
            sp.dma_start(wo_sb[:, :], wo).then_inc(const_in, 16)
            load_ffn(0)
            sp.dma_start(b1_rows[:, :], b1.rearrange("g (c p) -> (g c) p", p=P)).then_inc(bias_in, 16)
            sp.dma_start(b2_all[:, :], b2.rearrange("(o g) h -> o (g h)", o=1).to_broadcast([P, B * D])).then_inc(bias_in, 16)
            sp.dma_start(bo_all[:, :], bo.rearrange("(o d) -> o d", o=1).to_broadcast([P, D])).then_inc(bias_in, 16)
            sp.dma_start(x_sb[:, C:B * C, :], x_rows[:, C:B * C, :]).then_inc(x_in, 16)
            sp.wait_ge(filled, 2)
            sp.wait_ge(cleared, 5)
            sp.wait_ge(start_dve, 1)
            store_k()
            sp.wait_ge(qk_split, 3)
            store_q()
            sp.wait_ge(scratch_w, 96)
            for g in range(3):
                load_stack(g, 0)
            store_max(turn(0, "prologue", "max"), 0)
            batch(0, "first")
            with sp.Fori(1, B - 1) as b:
                batch(b, "middle")
            batch(B - 1, "last")
            store_u(B - 1, 2)
            store_u(B - 1, 3)
            load_heads(B - 1)
            store_rden(B - 1)
            load_rden(B - 1)
            store_y(B - 1, turn(B - 1, "last", "out") + 1)
            sp.wait_ge(y_out, 16 * B)


def kernel(L0_attn_x, L0_attn_Wq, L0_attn_Wk, L0_attn_Wv, L0_attn_Wo, L0_attn_bo, L0_ffn_W1, L0_ffn_b1, L0_ffn_W2,
           L0_ffn_b2):
    import concourse.bacc as bacc
    from concourse.bass_utils import run_bass_kernel_spmd

    half = HD // 2
    inv_freq = (1.0 / 10000.0 ** (np.arange(half, dtype=np.float32) / half)).astype(np.float32)
    angle = np.arange(T, dtype=np.float32)[:, None] * inv_freq[None, :]
    rope = np.concatenate([np.cos(angle), np.sin(angle)], axis=-1).astype(np.float32)
    arrays = {
        "x": L0_attn_x, "wq": L0_attn_Wq, "wk": L0_attn_Wk, "wv": L0_attn_Wv, "wo": L0_attn_Wo, "bo": L0_attn_bo,
        "w1": L0_ffn_W1, "b1": L0_ffn_b1, "w2": L0_ffn_W2, "b2": L0_ffn_b2,
        "rope16": np.tile(rope, (1, H)),
        "headmask": np.kron(np.eye(H, dtype=np.float32), np.ones((HD, HD), np.float32)),
        "identity": np.eye(P, dtype=np.float32),
    }
    arrays = {f"in_{n}": np.ascontiguousarray(a) for n, a in arrays.items()}
    nc = bacc.Bacc("TRN2", target_bir_lowering=False, num_devices=1)
    args = [nc.dram_tensor(n, a.shape, mybir.dt.from_np(a.dtype), kind="ExternalInput").ap() for n, a in arrays.items()]
    args.append(nc.dram_tensor("out_y", (B, T, D), F32, kind="ExternalOutput").ap())
    build(nc, *args)
    r = run_bass_kernel_spmd(nc, [arrays], core_ids=[0])
    return r.results[0]["out_y"]
```

```python
from contextlib import ExitStack

import numpy as np

import concourse.bass as bass
from concourse import mybir

F32 = mybir.dt.float32
BF16 = mybir.dt.bfloat16
ALU = mybir.AluOpType
ACT = mybir.ActivationFunctionType
AX_X = mybir.AxisListType.X

P = 128
B, T, D = 8, 512, 128
H, HD = 16, 8
C = T // P
GH = 4
NG = H // GH
FC = 512 // P
NP3 = 3
ROWS = NP3 * NP3 * HD
MAX_ROW = 96
EPS = 1e-5
ONES_PAIR = float(np.array([0x3F803F80], np.uint32).view(np.float32)[0])

TILES = H * C
ROUND = 3
LAG = 7
EARLY = 6
WARM = 28
V_COPIES = [(0, 0), (0, 1), (0, 2), (1, 0)]

START = ["xnT", "q", "k", "v", "gram", "wo2", "b1T", "w2T", "w12", "ffn"]
PROLOGUE = ["xnT", "max", "q", "k"]
MIDDLE = ["xnT", "q", "max0", "k", "v", "max1", "w2T", "w12", "max2", "ffn", "max3", "out"]
FIRST = ["max0", "v", "w2T", "max1", "w12", "max2", "ffn", "max3"]
LAST = ["max0", "max1", "max2", "out"]


def turn(b, kind, job):
    if kind == "prologue":
        return PROLOGUE.index(job)
    if kind == "first":
        return len(PROLOGUE) + FIRST.index(job)
    jobs = {"middle": MIDDLE, "last": LAST}[kind]
    return b * len(MIDDLE) + (len(PROLOGUE) + len(FIRST) - len(MIDDLE) + jobs.index(job))


def build(nc, x, wq, wk, wv, wo, bo, w1, b1, w2, b2, rope16, headmask, identity, out):
    with ExitStack() as ctx:
        def sb(name, shape, dt):
            return ctx.enter_context(nc.sbuf_tensor(name, shape, dt))

        def sem(name):
            return ctx.enter_context(nc.semaphore(name))

        ident = sb("ident", [P, P], F32)
        ident_b = sb("ident_b", [P, P], BF16)
        ones = sb("ones", [P, P], F32)
        rope_sb = sb("rope_sb", [P, C, P], F32)
        mask_sb = sb("mask_sb", [P, P], F32)
        gram = sb("gram", [P, P], F32)
        wq_sb = sb("wq_sb", [P, D], F32)
        wk_sb = sb("wk_sb", [P, D], F32)
        wv_sb = sb("wv_sb", [P, D], F32)
        wo_sb = sb("wo_sb", [P, D], F32)
        wo2 = sb("wo2", [P, D], F32)
        w1_sb = sb("w1_sb", [P, FC, D], F32)
        w2_sb = sb("w2_sb", [P, FC * P], F32)
        w2T = sb("w2T", [P, FC, D], F32)
        w12 = sb("w12", [P, D], F32)
        b1_rows = sb("b1_rows", [B * FC, P], F32)
        b1T = sb("b1T", [P, B * FC], F32)
        b1_now = sb("b1_now", [P, FC], F32)
        b1w2 = sb("b1w2", [P, FC, D], F32)
        b2_all = sb("b2_all", [P, B * D], F32)
        bo_all = sb("bo_all", [P, D], F32)
        bias = sb("bias", [P, D], F32)
        x_all = sb("x_all", [P, B * C * D], F32)
        stats = sb("stats", [P, B * C, 6], F32)
        mv = sb("mv", [P, B * C, 2], F32)
        rstd = sb("rstd", [P, B * C], F32)
        half = sb("half", [P, B * C], F32)
        xn = sb("xn", [P, C, D], F32)
        xnT = sb("xnT", [P, T], F32)
        qk_f = sb("qk_f", [P, 2, T], F32)
        qk_r = sb("qk_r", [P, 2, T], F32)
        parts = sb("parts", [P, 2, NP3, T], BF16)
        q_stack = sb("q_stack", [P, NG, GH, T], BF16)
        k_stack = sb("k_stack", [P, NG, GH, T], BF16)
        v_stage = sb("v_stage", [P, C, H, HD], F32)
        v_ones = sb("v_ones", [P, C, H, 32], F32)
        negmax = sb("negmax", [P, 2, GH * C], F32)
        zero16 = sb("zero16", [P, GH * C], F32)
        max_r = sb("max_r", [P, GH * C], F32)
        max_parts = sb("max_parts", [P, 2, P // (GH * C), GH * C], BF16)
        max_rows = sb("max_rows", [NP3 * GH * C, P], BF16)
        probs = sb("probs", [P, 2, GH, C, T], F32)
        u_sb = sb("u_sb", [P, NG, T], F32)
        heads = sb("heads", [P, T], F32)
        den = sb("den", [P, T // HD], F32)
        rden = sb("rden", [P, T // HD], F32)
        rden_all = sb("rden_all", [P, T], F32)
        headsn = sb("headsn", [P, T], F32)
        y_base = sb("y_base", [P, B * C * D], F32)
        y = sb("y", [P, C, D], F32)
        heads_t = sb("heads_t", [P, C, P], F32)
        rden_t = sb("rden_t", [P, 2, C, GH], F32)

        q_dram = nc.dram_tensor("q_scratch", [H, HD, NP3, NP3, T], BF16).ap()
        k_dram = nc.dram_tensor("k_scratch", [H, HD, NP3, NP3, T], BF16).ap()
        u_dram = nc.dram_tensor("u_scratch", [H, HD + 1, T], F32).ap()
        r_dram = nc.dram_tensor("r_scratch", [H, T], F32).ap()

        ps_m = ctx.enter_context(nc.psum_tensor("ps_m", [P, 3, T], F32))
        ps_e = ctx.enter_context(nc.psum_tensor("ps_e", [P, 3, T], F32))
        ps_u = ctx.enter_context(nc.psum_tensor("ps_u", [P, T], F32))
        ps_side = ctx.enter_context(nc.psum_tensor("ps_side", [P, T], F32))

        x0_in, x1_in, x_in, wqkv_in, ffn_in, const_in, bias_in = map(
            sem, ["x0_in", "x1_in", "x_in", "wqkv_in", "ffn_in", "const_in", "bias_in"])
        filled, cleared = sem("filled"), sem("cleared")
        ln_stat, ln_rstd, xn_ready = map(sem, ["ln_stat", "ln_rstd", "xn_ready"])
        start_mm, start_act, start_dve = sem("start_mm"), sem("start_act"), sem("start_dve")
        side_mm, side_evac = sem("side_mm"), sem("side_evac")
        qk_split, scratch_w = sem("qk_split"), sem("scratch_w")
        start_split = sem("start_split")
        start_scratch_q, start_scratch_k = sem("start_scratch_q"), sem("start_scratch_k")
        stack_in = [sem(f"stack_in{g}") for g in range(NG)]
        v_copied = sem("v_copied")
        b1_copied, b1w2_done = sem("b1_copied"), sem("b1w2_done")
        bias_done, base_done = sem("bias_done"), sem("base_done")
        m_ready, m_done, max_split = map(sem, ["m_ready", "m_done", "max_split"])
        max_in = [sem(f"max_in{g}") for g in range(NG)]
        e_ready, e_done, pv_done, u_done = map(sem, ["e_ready", "e_done", "pv_done", "u_done"])
        u_out = [sem(f"u_out{g}") for g in range(NG)]
        heads_in, den_in, rden_done, rden_out, rden_in, norm_done = map(
            sem, ["heads_in", "den_in", "rden_done", "rden_out", "rden_in", "norm_done"])
        y_out = sem("y_out")
        last_mm, last_copied_a, last_copied_v, last_norm, last_y = map(
            sem, ["last_mm", "last_copied_a", "last_copied_v", "last_norm", "last_y"])
        last_pv_done = sem("last_pv_done")

        block = ctx.enter_context(nc.Block())

        def tile_bank(r, tile):
            return (r * TILES + tile) % ROUND

        def ahead(b, r, s, i, kind):
            n = GH * s + i + LAG
            return kind != "last" or n < H, b + n // H, r + n // H, n // GH % NG, n % GH

        def last_done(b, kind, job):
            if kind == "first":
                return start_mm, START.index(job) + 1
            return side_mm, b * len(MIDDLE) + (len(PROLOGUE) + len(FIRST) - 2 * len(MIDDLE) + MIDDLE.index(job) + 2)

        start_bank = {"xnT": ps_side[:, :], "q": ps_m[:, 0, :], "k": ps_m[:, 1, :], "v": ps_m[:, 2, :],
                      "gram": ps_e[:, 0, :], "wo2": ps_e[:, 1, :], "b1T": ps_e[:, 2, :], "w2T": ps_u[:, :],
                      "w12": ps_e[:, 0, :], "ffn": ps_e[:, 1, :]}

        def started(job):
            return START.index(job) + 1

        @block.tensor
        def _(pe):
            def side(index):
                if not (isinstance(index, int) and index == 0):
                    pe.wait_ge(side_evac, index)

            def transpose4(bank, done, src):
                for c in range(4):
                    last = nc.tensor.transpose(bank[:, c * P:(c + 1) * P], src(c), ident[:, :])
                last.then_inc(done, 1)

            def job_xnT(b, bank, done):
                pe.wait_ge(xn_ready, 4 * b + 4)
                transpose4(bank, done, lambda c: xn[:, c, :])

            def job_project(bank, done, w):
                nc.tensor.matmul(bank, w[:, :], xnT[:, :], start=True, stop=True).then_inc(done, 1)

            def tokens_chunk(bank, lhsT, w, c):
                return nc.tensor.matmul(bank[:, c * D:(c + 1) * D], lhsT[:, c * P:(c + 1) * P], w[:, :],
                                        start=True, stop=True)

            def job_tokens(bank, done, lhsT, w):
                for c in range(C):
                    last = tokens_chunk(bank, lhsT, w, c)
                last.then_inc(done, 1)

            def job_w2T(b, bank, done):
                pe.wait_ge(ffn_in, 32 * b + 32)
                transpose4(bank, done, lambda c: w2_sb[:, c * P:(c + 1) * P])

            def w12_chunk(bank, c):
                nc.tensor.matmul(bank[:, 0:D], w1_sb[:, c, :], w2T[:, c, :], start=(c == 0), stop=(c == FC - 1))

            def b1w2_sum(b, bank, done):
                pe.wait_ge(b1w2_done, 3 * b + 3)
                nc.tensor.matmul(bank[:, D:2 * D], ones[:, :], b1w2[:, 0, :], start=True, stop=True).then_inc(done, 1)

            def job_w12(b, bank, done):
                for c in range(FC):
                    w12_chunk(bank, c)
                b1w2_sum(b, bank, done)

            def job_max(G, parity, index):
                side(index)
                pe.wait_ge(max_split, 4 * G + 4)
                nc.tensor.transpose(ps_side[:, 0:P // 2].bitcast(BF16),
                                    max_parts[:, parity, :, :].rearrange("p a n -> p (a n)"), ident_b[:, :]
                                    ).then_inc(side_mm, 1)

            def free_bank(done, b, tile):
                count = TILES * b + (tile - ROUND + 1)
                if not (isinstance(count, int) and count < 1):
                    pe.wait_ge(done, count)

            def m_tile(b, r, g, i, c):
                tile = GH * C * g + C * i + c
                free_bank(m_done, b, tile)
                nc.tensor.matmul(ps_m[:, tile_bank(r, tile), :], q_stack[0:MAX_ROW, g, i, c * P:(c + 1) * P],
                                 k_stack[0:MAX_ROW, g, i, :], start=True, stop=True).then_inc(m_ready, 1)

            def e_tile(b, r, g, i, c, tile):
                free_bank(e_done, b, tile)
                nc.tensor.matmul(ps_e[:, tile_bank(r, tile), :], k_stack[:, g, i, c * P:(c + 1) * P],
                                 q_stack[:, g, i, :], start=True, stop=True).then_inc(e_ready, 1)

            def pv_chunk(G, g, c):
                if c == 0:
                    pe.wait_ge(e_done, 16 * G + 16)
                    if not (isinstance(G, int) and G == 0):
                        pe.wait_ge(u_done, G)
                for j in range(GH):
                    last = nc.tensor.matmul(ps_u[32 * j:32 * j + 32, :], v_ones[:, c, GH * g + j, :],
                                            probs[:, g % 2, j, c, :], start=(c == 0), stop=(c == C - 1))
                last.then_inc(pv_done, 1)

            def last_pv(c):
                pe.wait_ge(e_done, TILES * (B - 1) + 16 * (NG - 1) + GH * (c + 1))
                for j in range(GH):
                    last = nc.tensor.matmul(ps_m[32 * j:32 * j + 32, 2, :], v_ones[:, c, GH * (NG - 1) + j, :],
                                            probs[:, (NG - 1) % 2, j, c, :], start=(c == 0), stop=(c == C - 1))
                last.then_inc(last_pv_done, 1)

            def untranspose(g):
                if g == 0:
                    pe.wait_ge(m_done, TILES * B)
                if g >= 2:
                    pe.wait_ge(last_norm, 2 * (g - 1))
                pe.wait_ge(u_done, 4 * (B - 1) + g + 1)
                for c in range(C):
                    if g == NG - 1 and c == 2:
                        pe.wait_ge(u_done, 4 * B + 1)
                    last = nc.tensor.transpose(ps_m[:, g % 2, c * P:(c + 1) * P], u_sb[:, g, c * P:(c + 1) * P],
                                               ident[:, :])
                last.then_inc(last_mm, 1)

            def step(b, r, s, kind, jobs):
                G = 4 * b + s
                do_pv = not (kind == "first" and s == 0)
                for i in range(GH):
                    do_m, b_m, r_m, g_m, i_m = ahead(b, r, s, i, kind)
                    if i == 0:
                        pe.wait_ge(max_in[s], 16 * b + 16)
                    if do_m and i_m == 0:
                        pe.wait_ge(stack_in[g_m], 32 * b_m + 32)
                    for c in range(2):
                        e_tile(b, r, s, i, c, GH * C * s + C * i + c)
                        if do_m:
                            m_tile(b_m, r_m, g_m, i_m, c)
                    if (i, 0) in jobs:
                        jobs[i, 0]()
                    if do_pv:
                        if s == 1:
                            pe.wait_ge(v_copied, 4 * b + (i + 1))
                        pv_chunk(G - 1, (s - 1) % NG, i)
                    if (i, 1) in jobs:
                        jobs[i, 1]()
                    for c in range(2, 4):
                        e_tile(b, r, s, i, c, GH * C * s + C * i + c)
                        if do_m:
                            m_tile(b_m, r_m, g_m, i_m, c)
                    if (i, 2) in jobs:
                        jobs[i, 2]()

            def last_step(jobs):
                b, s = B - 1, NG - 1
                pe.wait_ge(max_in[s], 16 * b + 16)
                for c in range(C):
                    for i in range(GH):
                        if i == 2:
                            pv_chunk(4 * b + s - 1, s - 1, c)
                        e_tile(b, b % ROUND, s, i, c, GH * C * s + GH * c + i)
                    if c in jobs:
                        jobs[c]()
                    if c > 0:
                        last_pv(c - 1)

            def batch(b, r, kind):
                def on_side(name, job, *args):
                    def run():
                        side(turn(b, kind, name))
                        job(*args)
                    return run

                side_bank, done = ps_side[:, :], side_mm

                def maxima(s):
                    return lambda: job_max(4 * b + s + 1, (s + 1) % 2, turn(b, kind, f"max{s}"))

                def output():
                    pe.wait_ge(norm_done, b)
                    job_tokens(side_bank, done, headsn, wo2)

                jobs = [{(1, 2): maxima(0)}, {(1, 2): maxima(1)}, {(1, 2): maxima(2)}, {}]
                if kind == "first":
                    jobs[0][2, 0] = on_side("v", job_tokens, side_bank, done, xnT, wv_sb)
                    jobs[0][3, 0] = on_side("w2T", job_w2T, b + 1, side_bank, done)
                if kind == "middle":
                    jobs[0][0, 2] = on_side("xnT", job_xnT, b + 1, side_bank, done)
                    jobs[0][1, 0] = on_side("q", job_project, side_bank, done, wq_sb)
                    jobs[0][3, 0] = on_side("k", job_project, side_bank, done, wk_sb)
                    jobs[1][1, 0] = on_side("v", job_tokens, side_bank, done, xnT, wv_sb)
                    jobs[1][2, 0] = on_side("w2T", job_w2T, b + 1, side_bank, done)
                if kind != "last":
                    jobs[1][3, 0] = on_side("w12", job_w12, b + 1, side_bank, done)
                    jobs[2][3, 0] = on_side("ffn", job_tokens, side_bank, done, xnT, w12)
                    jobs[3][1, 2] = maxima(3)
                else:
                    jobs[2][2, 0] = lambda: untranspose(0)
                if kind == "middle":
                    jobs[3][2, 0] = on_side("out", output)
                for s in range(NG - 1 if kind == "last" else NG):
                    step(b, r, s, kind, jobs[s])
                if kind == "last":
                    last_step({0: lambda: untranspose(1), 2: on_side("out", output)})

            at, done = start_bank, start_mm
            pe.wait_ge(cleared, 1)
            for _ in range(WARM):
                nc.tensor.matmul(ps_u[:, 0:2 * P], ones[:, 0:P // 2].bitcast(BF16), ones[:, :].bitcast(BF16),
                                 start=True, stop=True)
            pe.wait_ge(const_in, 16)
            for c in range(C):
                pe.wait_ge(xn_ready, c + 1)
                last = nc.tensor.transpose(at["xnT"][:, c * P:(c + 1) * P], xn[:, c, :], ident[:, :])
            last.then_inc(done, 1)
            pe.wait_ge(wqkv_in, 48)
            pe.wait_ge(start_act, 1)
            job_project(at["q"], done, wq_sb)
            job_project(at["k"], done, wk_sb)
            job_tokens(at["v"], done, xnT, wv_sb)
            pe.wait_ge(const_in, 64)
            for c in range(C):
                last = nc.tensor.matmul(at["gram"][:, 0:P], rope_sb[:, c, :], rope_sb[:, c, :],
                                        start=(c == 0), stop=(c == C - 1))
            last.then_inc(done, 1)
            pe.wait_ge(start_dve, 1)
            nc.tensor.matmul(at["wo2"][:, 0:D], gram[:, :], wo_sb[:, :], start=True, stop=True).then_inc(done, 1)
            pe.wait_ge(bias_in, 48)
            nc.tensor.transpose(at["b1T"][:, 0:B * FC], b1_rows[:, :], ident[0:B * FC, 0:B * FC]).then_inc(done, 1)
            job_w2T(0, at["w2T"], done)
            pe.wait_ge(start_act, 4)

            def m_head(n, between=lambda c: None):
                if n % GH == 0:
                    pe.wait_ge(stack_in[n // GH], 32)
                for c in range(C):
                    m_tile(0, 0, n // GH, n % GH, c)
                    between(c)

            def start_ffn(c):
                mm = tokens_chunk(at["ffn"], xnT, w12, c)
                if c == C - 1:
                    mm.then_inc(done, 1)

            def next_xnT(c):
                mm = nc.tensor.transpose(ps_side[:, c * P:(c + 1) * P], xn[:, c, :], ident[:, :])
                if c == C - 1:
                    mm.then_inc(side_mm, 1)

            def first_max(c):
                if c == 0:
                    pe.wait_ge(start_dve, 2)
                    job_max(0, 0, turn(0, "prologue", "max"))

            m_head(0)
            pe.wait_ge(start_act, 7)
            m_head(1, lambda c: w12_chunk(at["w12"], c))
            b1w2_sum(0, at["w12"], done)
            m_head(2)
            pe.wait_ge(start_act, 8)
            m_head(3, start_ffn)
            pe.wait_ge(xn_ready, 8)
            m_head(4, next_xnT)
            m_head(5, first_max)
            side(turn(0, "prologue", "q"))
            job_project(ps_side[:, :], side_mm, wq_sb)
            m_head(6)
            side(turn(0, "prologue", "k"))
            job_project(ps_side[:, :], side_mm, wk_sb)
            pe.wait_ge(start_act, 9)
            batch(0, 0, "first")
            with pe.Fori(1, B - ROUND, ROUND) as b:
                for n in range(ROUND):
                    batch(b + n, (1 + n) % ROUND, "middle")
            batch(B - 1, (B - 1) % ROUND, "last")
            last_pv(C - 1)
            untranspose(NG - 2)
            untranspose(NG - 1)
            pe.wait_ge(last_norm, 2 * NG)
            for c in range(C):
                last = nc.tensor.transpose(ps_m[:, c // 2 * 2, c * P:(c + 1) * P], heads_t[:, c, :], ident[:, :])
                if c % 2:
                    last.then_inc(last_mm, 1)
            for c in range(C):
                if c % 2 == 0:
                    pe.wait_ge(last_copied_a if c == 0 else last_copied_v, 1)
                half_bank = ps_side if c < 2 else ps_u
                last = nc.tensor.matmul(half_bank[:, c * D:(c + 1) * D], headsn[:, c * P:(c + 1) * P], wo2[:, :],
                                        start=True, stop=True)
                if c % 2:
                    last.then_inc(last_mm, 1)

        @block.scalar
        def _(act):
            def evac(index, pairs):
                act.wait_ge(side_mm, index + 1)
                for dst, src in pairs:
                    last = nc.scalar.activation(dst, src, ACT.Copy)
                last.then_inc(side_evac, 1)

            def evac_qk(b, index, o):
                act.wait_ge(scratch_w, 96 * b)
                evac(index, [(qk_f[:, o, :], ps_side[:, :]), (parts[:, o, 0, :], ps_side[:, :])])

            def evac_v(b, index):
                act.wait_ge(v_copied, 4 * b)
                evac(index, [(v_stage[:, :, :, :].rearrange("p c h d -> p (c h d)"), ps_side[:, :])])

            def copy_v(c):
                nc.scalar.activation(v_ones[:, c, :, 0:HD], v_stage[:, c, :, :], ACT.Copy).then_inc(v_copied, 1)

            def evac_max(b, s, index):
                if not (isinstance(b, int) and b == 0 and s == 0):
                    before = b if s > 0 else b - 1
                    act.wait_ge(max_in[(s - 1) % NG], 16 * before + 16)
                evac(index, [(max_rows[:, :], ps_side[0:NP3 * GH * C, 0:P // 2].bitcast(BF16))])

            def evac_u(b, G, g):
                act.wait_ge(pv_done, 4 * G + 4)
                if not (isinstance(b, int) and b == 0):
                    act.wait_ge(u_out[g], 64 * b)
                nc.scalar.activation(u_sb[:, g, :], ps_u[:, :], ACT.Copy).then_inc(u_done, 1)

            def exp_tile(r, s, i, c, tile):
                nc.scalar.activation(probs[:, s % 2, i, c, :], ps_e[:, tile_bank(r, tile), :], ACT.Exp,
                                     scale=float(HD) ** -0.5).then_inc(e_done, 1)

            def step(b, r, s, kind, jobs):
                G = 4 * b + s
                for i in range(GH):
                    for c in range(C):
                        if c == 2:
                            for place in range(2):
                                if (i, place) in jobs:
                                    jobs[i, place]()
                            if i == GH - 1 and not (kind == "first" and s == 0):
                                evac_u(b if s > 0 else b - 1, G - 1, (s - 1) % NG)
                        if c == 3 and (s, i) in V_COPIES and kind != "first":
                            n = V_COPIES.index((s, i))
                            act.wait_ge(pv_done, 16 * b + (n - 3))
                            copy_v(n)
                        act.wait_ge(e_ready, 16 * G + (4 * i + c + 1))
                        exp_tile(r, s, i, c, GH * C * s + C * i + c)
                    if (i, 2) in jobs:
                        jobs[i, 2]()

            def last_step():
                G, s = 4 * B - 1, NG - 1
                for c in range(C):
                    for i in range(GH):
                        if c == C - 1 and i == 2:
                            evac_u(B - 1, G - 1, s - 1)
                        act.wait_ge(e_ready, 16 * G + (GH * c + i + 1))
                        exp_tile((B - 1) % ROUND, s, i, c, GH * C * s + GH * c + i)

            def batch(b, r, kind):
                t = lambda job: turn(b, kind, job)
                jobs = [{(1, 2): lambda: evac_max(b, 1, t("max0"))}, {(1, 2): lambda: evac_max(b, 2, t("max1"))},
                        {(1, 2): lambda: evac_max(b, 3, t("max2"))}, {}]
                evac_w2T = lambda: evac(t("w2T"), [(w2T[:, :, :].rearrange("p c h -> p (c h)"), ps_side[:, :])])
                if kind == "first":
                    jobs[0][2, 0] = lambda: evac_v(b + 1, t("v"))
                    jobs[0][3, 0] = evac_w2T
                if kind == "middle":
                    jobs[0][0, 2] = lambda: evac(t("xnT"), [(xnT[:, :], ps_side[:, :])])
                    jobs[0][1, 0] = lambda: evac_qk(b + 1, t("q"), 0)
                    jobs[0][3, 0] = lambda: evac_qk(b + 1, t("k"), 1)
                    jobs[1][1, 0] = lambda: evac_v(b + 1, t("v"))
                    jobs[1][2, 0] = evac_w2T
                if kind != "last":
                    jobs[3][1, 2] = lambda: evac_max(b + 1, 0, t("max3"))
                for s in range(NG - 1 if kind == "last" else NG):
                    step(b, r, s, kind, jobs[s])
                if kind == "last":
                    last_step()

            def start_evac(job, pairs):
                act.wait_ge(start_mm, started(job))
                for dst, src in pairs:
                    last = nc.scalar.activation(dst, src, ACT.Copy)
                last.then_inc(start_act, 1)

            act.wait_ge(cleared, 3)
            nc.scalar.activation(q_stack[64:P, :, :, :].rearrange("p g i t -> p (g i t)").bitcast(F32),
                                 zero16[64:P, 0:1].to_broadcast([P - 64, NG * GH * T // 2]), ACT.Copy
                                 ).then_inc(cleared, 1)
            at = start_bank
            start_evac("xnT", [(xnT[:, :], at["xnT"])])
            start_evac("q", [(parts[:, 0, 0, :], at["q"])])
            start_evac("k", [(parts[:, 1, 0, :], at["k"])])
            start_evac("v", [(v_stage[:, :, :, :].rearrange("p c h d -> p (c h d)"), at["v"])])
            act.wait_ge(filled, 1)
            act.wait_ge(start_act, 4)
            for c in range(C):
                copy_v(c)
            start_evac("wo2", [(wo2[:, :], at["wo2"][:, 0:D])])
            start_evac("b1T", [(b1T[:, :], at["b1T"][:, 0:B * FC])])
            start_evac("w2T", [(w2T[:, :, :].rearrange("p c h -> p (c h)"), at["w2T"])])
            start_evac("w12", [(w12[:, :], at["w12"][:, 0:D]), (bias[:, :], at["w12"][:, D:2 * D])])
            start_evac("ffn", [(y_base[:, 0:C * D], at["ffn"])])
            evac(turn(0, "prologue", "xnT"), [(xnT[:, :], ps_side[:, :])])
            evac_max(0, 0, turn(0, "prologue", "max"))
            evac_qk(1, turn(0, "prologue", "q"), 0)
            evac_qk(1, turn(0, "prologue", "k"), 1)
            batch(0, 0, "first")
            with act.Fori(1, B - ROUND, ROUND) as b:
                for n in range(ROUND):
                    batch(b + n, (1 + n) % ROUND, "middle")
            batch(B - 1, (B - 1) % ROUND, "last")
            act.wait_ge(last_pv_done, C)
            act.wait_ge(u_out[NG - 1], 64 * (B - 1))
            for n in range(2):
                columns = slice(n * T // 2, (n + 1) * T // 2)
                nc.scalar.activation(u_sb[:, NG - 1, columns], ps_m[:, 2, columns], ACT.Copy).then_inc(u_done, 1)
            act.wait_ge(last_mm, NG + 1)
            nc.scalar.activation(headsn[:, 0:T // 2], ps_m[:, 0, 0:T // 2], ACT.Copy).then_inc(last_copied_a, 1)

        @block.vector
        def _(dve):
            def stat(c0, c1):
                for c in range(c0, c1):
                    last = nc.vector.bn_stats(stats[:, c, :], x_all[:, c * D:(c + 1) * D])
                last.then_inc(ln_stat, 1)

            def aggregate(c0, c1, count):
                dve.wait_ge(ln_stat, count)
                for c in range(c0, c1):
                    last = nc.vector.bn_aggr(mv[:, c, :], stats[:, c, :])
                last.then_inc(ln_stat, 1)

            def normalise(b, kind):
                dve.wait_ge(*last_done(b, kind, "xnT"))
                for c in range(C):
                    nc.vector.tensor_scalar(xn[:, c, :], x_all[:, bass.ds(b * (C * D) + (C + c) * D, D)],
                                            mv[:, bass.ds(b * C + (C + c), 1), 0], rstd[:, bass.ds(b * C + (C + c), 1)],
                                            ALU.subtract, ALU.mult).then_inc(xn_ready, 1)

            def reduce_tile(b, r, g, i, c):
                tile = GH * C * g + C * i + c
                dve.wait_ge(m_ready, TILES * b + (tile + 1))
                nc.vector.tensor_reduce(negmax[:, g % 2, C * i + c:C * i + c + 1], ps_m[:, tile_bank(r, tile), :],
                                        AX_X, ALU.max, negate=True).then_inc(m_done, 1)

            def reciprocals(b):
                dve.wait_ge(den_in, 16 * b + 16)
                if not (isinstance(b, int) and b == 0):
                    dve.wait_ge(rden_out, 16 * b)
                nc.vector.reciprocal(rden[:, :], den[:, :]).then_inc(rden_done, 1)

            def finish(b, index):
                dve.wait_ge(base_done, b + 1)
                dve.wait_ge(side_mm, index + 1)
                if not (isinstance(b, int) and b == 0):
                    dve.wait_ge(y_out, 16 * b)
                nc.vector.tensor_tensor(y[:, :, :].rearrange("p c d -> p (c d)"), ps_side[:, :],
                                        y_base[:, bass.ds(b * (C * D), C * D)], ALU.add).then_inc(side_evac, 1)

            def normalise_group(g):
                dve.wait_ge(last_mm, g + 1)
                sums = ps_m[:, g % 2, :].rearrange("p (c j r) -> p c j r", c=C, j=GH)
                nc.vector.reciprocal(rden_t[:, g % 2, :, :], sums[:, :, :, HD]).then_inc(last_norm, 1)
                dve.wait_ge(last_norm, 2 * g + 1)
                nc.vector.tensor_tensor(
                    heads_t[:, :, :].rearrange("p c (g j d) -> p c g j d", g=NG, j=GH)[:, :, g, :, :],
                    sums[:, :, :, 0:HD],
                    rden_t[:, g % 2, :, :].rearrange("p c (j o) -> p c j o", o=1).to_broadcast([P, C, GH, HD]),
                    ALU.mult).then_inc(last_norm, 1)

            def evac_w12(b, bank, done):
                dve.wait_ge(base_done, b)
                nc.vector.tensor_copy(w12[:, :], bank[:, 0:D])
                nc.vector.tensor_tensor(bias[:, :], bank[:, D:2 * D], b2_all[:, bass.ds(b * D, D)],
                                        ALU.add).then_inc(done, 1)

            def evac_ffn(b, bank, done):
                nc.vector.tensor_tensor(y_base[:, bass.ds(b * (C * D), C * D)], bank,
                                        x_all[:, bass.ds(b * (C * D), C * D)], ALU.add).then_inc(done, 1)

            def step(b, r, s, kind, jobs):
                for i in range(GH):
                    do_m, b_m, r_m, g_m, i_m = ahead(b, r, s, i, kind)
                    for c in range(C):
                        if do_m:
                            reduce_tile(b_m, r_m, g_m, i_m, c)
                        if c % 2 and (i, c // 2) in jobs:
                            jobs[i, c // 2]()

            def batch(b, r, kind):
                t = lambda job: turn(b, kind, job)

                def side_w12():
                    dve.wait_ge(side_mm, t("w12") + 1)
                    evac_w12(b + 1, ps_side[:, :], side_evac)

                def side_ffn():
                    dve.wait_ge(side_mm, t("ffn") + 1)
                    evac_ffn(b + 1, ps_side[:, :], side_evac)

                def statistics(n):
                    def run():
                        if n == 0:
                            dve.wait_ge(x_in, 32)
                        c = EARLY * C + 2 * n
                        stat(c, c + 2)
                        aggregate(c, c + 2, 2 * n + 7)
                    return run

                jobs = [{} for _ in range(NG)]
                if kind == "first":
                    for n in range((B - EARLY) * C // 2):
                        jobs[2][n, 1] = statistics(n)
                else:
                    jobs[2][1, 0] = lambda: reciprocals(b - 1)
                    jobs[3][2, 0] = lambda: finish(b - 1, t("out"))
                if kind != "last":
                    jobs[1][3, 0] = side_w12
                    jobs[2][3, 0] = side_ffn
                if kind == "middle":
                    normalise(b, kind)
                for s in range(NG):
                    if kind == "last" and s == NG - 1:
                        normalise_group(0)
                        normalise_group(1)
                    step(b, r, s, kind, jobs[s])

            nc.vector.memset(ones[:, :], 1.0).then_inc(cleared, 1)
            nc.vector.memset(half[:, :], -0.5).then_inc(cleared, 1)
            nc.vector.memset(zero16[:, :], 0.0).then_inc(cleared, 1)
            nc.vector.memset(max_parts[:, :, :, :], 0.0).then_inc(cleared, 1)
            dve.wait_ge(x0_in, 16)
            stat(0, C)
            aggregate(0, C, 1)
            dve.wait_ge(ln_rstd, 2)
            for c in range(C):
                nc.vector.tensor_scalar(xn[:, c, :], x_all[:, c * D:(c + 1) * D], mv[:, c:c + 1, 0], rstd[:, c:c + 1],
                                        ALU.subtract, ALU.mult).then_inc(xn_ready, 1)
            at = start_bank
            for o, job in enumerate(("q", "k")):
                dve.wait_ge(start_act, 2 + o)
                nc.vector.tensor_tensor(qk_r[:, o, :], at[job], parts[:, o, 0, :],
                                        ALU.subtract).then_inc(start_split, 1)
                dve.wait_ge(start_split, 3 * o + 1)
                nc.vector.tensor_copy(parts[:, o, 1, :], qk_r[:, o, :]).then_inc(start_split, 1)
                dve.wait_ge(start_split, 3 * o + 2)
                nc.vector.tensor_tensor(parts[:, o, 2, :], qk_r[:, o, :], parts[:, o, 1, :],
                                        ALU.subtract).then_inc(start_split, 1)
            dve.wait_ge(start_mm, started("gram"))
            dve.wait_ge(const_in, 64)
            nc.vector.tensor_tensor(gram[:, :], at["gram"][:, 0:P], mask_sb[:, :], ALU.mult).then_inc(start_dve, 1)
            nc.vector.tensor_copy(ident_b[:, :], ident[:, :]).then_inc(start_dve, 1)
            dve.wait_ge(x1_in, 16)
            stat(C, 2 * C)
            aggregate(C, 2 * C, 3)
            dve.wait_ge(x_in, 16)
            stat(2 * C, EARLY * C)
            aggregate(2 * C, EARLY * C, 5)
            dve.wait_ge(ln_rstd, 4)
            normalise(0, "first")
            for n in range(LAG):
                for c in range(C):
                    reduce_tile(0, 0, n // GH, n % GH, c)
            batch(0, 0, "first")
            dve.wait_ge(ln_rstd, 8)
            with dve.Fori(1, B - ROUND, ROUND) as b:
                for n in range(ROUND):
                    batch(b + n, (1 + n) % ROUND, "middle")
            batch(B - 1, (B - 1) % ROUND, "last")
            dve.wait_ge(base_done, B)
            normalise_group(NG - 2)
            normalise_group(NG - 1)
            dve.wait_ge(last_mm, NG + 2)
            nc.vector.tensor_copy(headsn[:, T // 2:T], ps_m[:, 2, T // 2:T]).then_inc(last_copied_v, 1)
            for n in range(2):
                dve.wait_ge(last_mm, NG + 3 + n)
                if n == 0:
                    dve.wait_ge(y_out, 16 * (B - 1))
                nc.vector.tensor_tensor(y[:, 2 * n:2 * n + 2, :].rearrange("p c d -> p (c d)"),
                                        (ps_side, ps_u)[n][:, n * 2 * D:(n + 1) * 2 * D],
                                        y_base[:, ((B - 1) * C + 2 * n) * D:((B - 1) * C + 2 * n + 2) * D],
                                        ALU.add).then_inc(last_y, 1)

        @block.gpsimd
        def _(pool):
            def split_qk(count, o):
                nc.gpsimd.tensor_tensor(parts[:, o, 1, :], qk_f[:, o, :], parts[:, o, 0, :],
                                        ALU.subtract).then_inc(qk_split, 1)
                nc.gpsimd.tensor_tensor(qk_r[:, o, :], qk_f[:, o, :], parts[:, o, 0, :],
                                        ALU.subtract).then_inc(qk_split, 1)
                pool.wait_ge(qk_split, count + 2)
                nc.gpsimd.tensor_tensor(parts[:, o, 2, :], qk_r[:, o, :], parts[:, o, 1, :],
                                        ALU.subtract).then_inc(qk_split, 1)

            def split_max(G, parity):
                pool.wait_ge(m_done, 16 * G + 16)
                nc.gpsimd.tensor_tensor(max_parts[:, parity, 0, :], negmax[:, parity, :], zero16[:, :],
                                        ALU.add).then_inc(max_split, 1)
                pool.wait_ge(max_split, 4 * G + 1)
                nc.gpsimd.tensor_tensor(max_parts[:, parity, 1, :], negmax[:, parity, :], max_parts[:, parity, 0, :],
                                        ALU.subtract).then_inc(max_split, 1)
                nc.gpsimd.tensor_tensor(max_r[:, :], negmax[:, parity, :], max_parts[:, parity, 0, :],
                                        ALU.subtract).then_inc(max_split, 1)
                pool.wait_ge(max_split, 4 * G + 3)
                nc.gpsimd.tensor_tensor(max_parts[:, parity, 2, :], max_r[:, :], max_parts[:, parity, 1, :],
                                        ALU.subtract).then_inc(max_split, 1)

            def multiply_b1(b):
                pool.wait_ge(b1_copied, b + 1)
                nc.gpsimd.tensor_tensor(b1w2[:, :, :], w2T[:, :, :],
                                        b1_now[:, :].rearrange("p (c o) -> p c o", o=1).to_broadcast([P, FC, D]),
                                        ALU.mult).then_inc(b1w2_done, 1)
                pool.wait_ge(b1w2_done, 3 * b + 1)
                nc.gpsimd.tensor_tensor(b1w2[:, 0:2, :], b1w2[:, 0:2, :], b1w2[:, 2:4, :],
                                        ALU.add).then_inc(b1w2_done, 1)
                pool.wait_ge(b1w2_done, 3 * b + 2)
                nc.gpsimd.tensor_tensor(b1w2[:, 0, :], b1w2[:, 0, :], b1w2[:, 1, :], ALU.add).then_inc(b1w2_done, 1)

            def copy_b1(b):
                nc.gpsimd.tensor_copy(b1_now[:, :], b1T[:, bass.ds(b * FC, FC)]).then_inc(b1_copied, 1)

            def inverse_std(c0, c1, stat_count, rstd_count):
                pool.wait_ge(ln_stat, stat_count)
                nc.gpsimd.tensor_scalar(rstd[:, c0:c1], mv[:, c0:c1, 1], 1.0, EPS,
                                        ALU.mult, ALU.add).then_inc(ln_rstd, 1)
                pool.wait_ge(ln_rstd, rstd_count)
                nc.gpsimd.tensor_tensor(rstd[:, c0:c1], rstd[:, c0:c1], half[:, c0:c1], ALU.pow).then_inc(ln_rstd, 1)

            def add_bias(b):
                rows = y_base[:, bass.ds(b * (C * D), C * D)].rearrange("p (c d) -> p c d", c=C)
                nc.gpsimd.tensor_tensor(rows, rows,
                                        bias[:, :].rearrange("p (o d) -> p o d", o=1).to_broadcast([P, C, D]),
                                        ALU.add).then_inc(base_done, 1)

            def norm(b):
                pool.wait_ge(heads_in, 16 * b + 16)
                pool.wait_ge(rden_in, 16 * b + 16)
                nc.gpsimd.tensor_tensor(headsn[:, :], heads[:, :], rden_all[:, :], ALU.mult).then_inc(norm_done, 1)

            def batch(b, r, kind):
                t = lambda job: turn(b, kind, job)
                split_max(4 * b + 1, 1)
                if kind != "last":
                    for o, job in enumerate(("q", "k")):
                        pool.wait_ge(side_evac, (turn(0, "prologue", job) if kind == "first" else t(job)) + 1)
                        split_qk(6 * b + 3 * o, o)
                    copy_b1(b + 1)
                split_max(4 * b + 2, 0)
                if kind != "last":
                    pool.wait_ge(side_evac, t("w2T") + 1)
                    multiply_b1(b + 1)
                split_max(4 * b + 3, 1)
                if kind != "last":
                    pool.wait_ge(side_evac, t("ffn") + 1)
                    add_bias(b + 1)
                    split_max(4 * b + 4, 0)
                if kind != "first":
                    norm(b - 1)
                else:
                    inverse_std(EARLY * C, B * C, 6 + (B - EARLY) * C, 7)

            nc.gpsimd.memset(v_ones[:, :, :, :], 1.0).then_inc(filled, 1)
            pool.wait_ge(filled, 1)
            pool.wait_ge(cleared, 4)
            inverse_std(0, C, 2, 1)
            pool.wait_ge(ln_rstd, 2)
            nc.gpsimd.memset(k_stack[64:P, :, :, :].rearrange("p g i t -> p (g i t)").bitcast(F32),
                             ONES_PAIR).then_inc(filled, 1)
            pool.wait_ge(filled, 2)
            inverse_std(C, 2 * C, 4, 3)
            pool.wait_ge(bias_in, 48)
            b2_rows = b2_all[:, :].rearrange("p (g d) -> p g d", g=B)
            nc.gpsimd.tensor_tensor(b2_rows, b2_rows,
                                    bo_all[:, :].rearrange("p (o d) -> p o d", o=1).to_broadcast([P, B, D]),
                                    ALU.add).then_inc(bias_done, 1)
            pool.wait_ge(start_act, 6)
            copy_b1(0)
            pool.wait_ge(start_act, 7)
            multiply_b1(0)
            split_max(0, 0)
            pool.wait_ge(bias_done, 1)
            pool.wait_ge(start_act, 8)
            nc.gpsimd.tensor_tensor(bias[:, :], bias[:, :], b2_all[:, 0:D], ALU.add).then_inc(bias_done, 1)
            pool.wait_ge(start_act, 9)
            nc.gpsimd.tensor_tensor(y_base[:, 0:C * D], y_base[:, 0:C * D], x_all[:, 0:C * D],
                                    ALU.add).then_inc(bias_done, 1)
            pool.wait_ge(bias_done, 3)
            add_bias(0)
            inverse_std(2 * C, EARLY * C, 6, 5)
            batch(0, 0, "first")
            with pool.Fori(1, B - ROUND, ROUND) as b:
                for n in range(ROUND):
                    batch(b + n, (1 + n) % ROUND, "middle")
            batch(B - 1, (B - 1) % ROUND, "last")

        @block.sync
        def _(sp):
            def load_rows(stack, scratch, g):
                sp.dma_start(stack[0:ROWS, g, :, :], scratch[GH * g:GH * g + GH].rearrange("h d a e t -> (d a e) h t")
                             ).then_inc(stack_in[g], 16)

            def load_stack(g):
                load_rows(q_stack, q_dram, g)
                load_rows(k_stack, k_dram, g)

            def load_ffn(b):
                sp.dma_start(w1_sb[:, :, :], w1[b, :, :].rearrange("(c p) h -> p c h", p=P)).then_inc(ffn_in, 16)
                sp.dma_start(w2_sb[:, :], w2[b, :, :]).then_inc(ffn_in, 16)

            def store_q(h0, h1, done):
                for e in range(NP3):
                    sp.dma_start(q_dram[h0:h1, :, :, e, :].rearrange("h d a t -> (h d) a t"),
                                 parts[h0 * HD:h1 * HD, 0, :, :]).then_inc(done, 16)

            def store_k(h0, h1, done):
                for a in range(NP3):
                    sp.dma_start(k_dram[h0:h1, :, a, :, :].rearrange("h d e t -> (h d) e t"),
                                 parts[h0 * HD:h1 * HD, 1, :, :]).then_inc(done, 16)

            def store_max(index, g):
                sp.wait_ge(side_evac, index + 1)
                sp.dma_start(q_stack[MAX_ROW:MAX_ROW + NP3, g, :, :].rearrange("a i (c t) -> a (i c) t", c=C),
                             max_rows[:, :]).then_inc(max_in[g], 16)

            def store_u(b, g):
                sp.wait_ge(u_done, 4 * b + (g + 1))
                for j in range(GH):
                    sp.dma_start(u_dram[GH * g + j, :, :], u_sb[32 * j:32 * j + HD + 1, g, :]).then_inc(u_out[g], 16)

            def load_heads(b):
                for g in range(NG):
                    sp.wait_ge(u_out[g], 64 * b + 64)
                if not (isinstance(b, int) and b == 0):
                    sp.wait_ge(norm_done, b)
                sp.dma_start(den[:, :], u_dram[:, HD, :].rearrange("h (k t) -> h k t", k=HD)).then_inc(den_in, 16)
                sp.dma_start(heads[:, :], u_dram[:, 0:HD, :]).then_inc(heads_in, 16)

            def store_rden(b):
                sp.wait_ge(rden_done, b + 1)
                sp.dma_start(r_dram.rearrange("h (k t) -> (h k) t", k=HD), rden[:, :]).then_inc(rden_out, 16)

            def load_rden(b):
                sp.wait_ge(rden_out, 16 * b + 16)
                sp.dma_start(rden_all[:, :], r_dram.rearrange("h (o t) -> h o t", o=1).to_broadcast([H, HD, T])
                             ).then_inc(rden_in, 16)

            def store_y(b, index):
                sp.wait_ge(side_evac, index + 1)
                sp.dma_start(out[b, :, :].rearrange("(c p) d -> p c d", p=P), y[:, :, :]).then_inc(y_out, 16)

            def batch(b, r, kind):
                first, last = kind == "first", kind == "last"
                t = lambda job: turn(b, kind, job)
                if not first:
                    sp.wait_ge(e_ready, 64 * b)
                load_stack(3)
                if not last:
                    sp.wait_ge(*last_done(b, kind, "w12"))
                    load_ffn(b + 1)
                if not first:
                    store_u(b - 1, 2)
                store_max(t("max0"), 1)
                if not last:
                    sp.wait_ge(stack_in[3], 32 * b + 32)
                    sp.wait_ge(qk_split, 6 * b + 3)
                    store_q(0, H, scratch_w)
                    sp.wait_ge(qk_split, 6 * b + 6)
                    store_k(0, H, scratch_w)
                if not first:
                    store_u(b - 1, 3)
                store_max(t("max1"), 2)
                if not last:
                    sp.wait_ge(scratch_w, 96 * b + 192)
                    load_stack(0)
                if not first:
                    load_heads(b - 1)
                if not last:
                    sp.wait_ge(e_ready, 64 * b + 32)
                    load_stack(1)
                if not first:
                    sp.wait_ge(heads_in, 16 * b)
                    sp.wait_ge(den_in, 16 * b)
                if not last:
                    store_u(b, 0)
                store_max(t("max2"), 3)
                if not first:
                    store_rden(b - 1)
                    load_rden(b - 1)
                if not last:
                    sp.wait_ge(e_ready, 64 * b + 48)
                    load_stack(2)
                if not last:
                    store_u(b, 1)
                    store_max(t("max3"), 0)
                if not first:
                    store_y(b - 1, turn(b, kind, "out"))

            x_rows = x.rearrange("b (c p) d -> p (b c) d", p=P)
            x_sb = x_all[:, :].rearrange("p (n d) -> p n d", d=D)
            sp.dma_start(x_sb[:, 0:C, :], x_rows[:, 0:C, :]).then_inc(x0_in, 16)
            sp.dma_start(ident[:, :], identity).then_inc(const_in, 16)
            for dst, src in ((wq_sb, wq), (wk_sb, wk), (wv_sb, wv)):
                sp.dma_start(dst[:, :], src).then_inc(wqkv_in, 16)
            sp.wait_ge(const_in, 16)
            sp.dma_start(rope_sb[:, :, :], rope16.rearrange("(c p) n -> p c n", p=P)).then_inc(const_in, 16)
            sp.dma_start(mask_sb[:, :], headmask).then_inc(const_in, 16)
            sp.dma_start(wo_sb[:, :], wo).then_inc(const_in, 16)
            load_ffn(0)
            sp.dma_start(b1_rows[:, :], b1.rearrange("g (c p) -> (g c) p", p=P)).then_inc(bias_in, 16)
            sp.dma_start(b2_all[:, :], b2.rearrange("(o g) h -> o (g h)", o=1).to_broadcast([P, B * D])
                         ).then_inc(bias_in, 16)
            sp.dma_start(bo_all[:, :], bo.rearrange("(o d) -> o d", o=1).to_broadcast([P, D])).then_inc(bias_in, 16)
            sp.dma_start(x_sb[:, C:2 * C, :], x_rows[:, C:2 * C, :]).then_inc(x1_in, 16)
            sp.dma_start(x_sb[:, 2 * C:EARLY * C, :], x_rows[:, 2 * C:EARLY * C, :]).then_inc(x_in, 16)
            sp.wait_ge(filled, 2)
            sp.wait_ge(cleared, 5)
            sp.wait_ge(start_split, 3)
            store_q(0, GH, start_scratch_q)
            sp.wait_ge(start_split, 6)
            store_k(0, GH, start_scratch_k)
            sp.wait_ge(start_scratch_q, 48)
            load_rows(q_stack, q_dram, 0)
            sp.wait_ge(start_scratch_k, 48)
            load_rows(k_stack, k_dram, 0)
            store_q(GH, H, scratch_w)
            store_k(GH, H, scratch_w)
            sp.wait_ge(scratch_w, 96)
            for g in range(1, 3):
                load_stack(g)
            sp.wait_ge(x_in, 16)
            sp.dma_start(x_sb[:, EARLY * C:B * C, :], x_rows[:, EARLY * C:B * C, :]).then_inc(x_in, 16)
            store_max(turn(0, "prologue", "max"), 0)
            batch(0, 0, "first")
            with sp.Fori(1, B - ROUND, ROUND) as b:
                for n in range(ROUND):
                    batch(b + n, (1 + n) % ROUND, "middle")
            batch(B - 1, (B - 1) % ROUND, "last")
            for n in range(2):
                sp.wait_ge(last_y, n + 1)
                sp.dma_start(out[B - 1, n * 2 * P:(n + 1) * 2 * P, :].rearrange("(c p) d -> p c d", p=P),
                             y[:, 2 * n:2 * n + 2, :]).then_inc(y_out, 16)
            sp.wait_ge(y_out, 16 * B + 16)


def kernel(L0_attn_x, L0_attn_Wq, L0_attn_Wk, L0_attn_Wv, L0_attn_Wo, L0_attn_bo, L0_ffn_W1, L0_ffn_b1, L0_ffn_W2,
           L0_ffn_b2):
    import concourse.bacc as bacc
    from concourse.bass_utils import run_bass_kernel_spmd

    half = HD // 2
    inv_freq = (1.0 / 10000.0 ** (np.arange(half, dtype=np.float32) / half)).astype(np.float32)
    angle = np.arange(T, dtype=np.float32)[:, None] * inv_freq[None, :]
    rope = np.concatenate([np.cos(angle), np.sin(angle)], axis=-1).astype(np.float32)
    arrays = {
        "x": L0_attn_x, "wq": L0_attn_Wq, "wk": L0_attn_Wk, "wv": L0_attn_Wv, "wo": L0_attn_Wo, "bo": L0_attn_bo,
        "w1": L0_ffn_W1, "b1": L0_ffn_b1, "w2": L0_ffn_W2, "b2": L0_ffn_b2,
        "rope16": np.tile(rope, (1, H)),
        "headmask": np.kron(np.eye(H, dtype=np.float32), np.ones((HD, HD), np.float32)),
        "identity": np.eye(P, dtype=np.float32),
    }
    arrays = {f"in_{n}": np.ascontiguousarray(a) for n, a in arrays.items()}
    nc = bacc.Bacc("TRN2", target_bir_lowering=False, num_devices=1)
    args = [nc.dram_tensor(n, a.shape, mybir.dt.from_np(a.dtype), kind="ExternalInput").ap() for n, a in arrays.items()]
    args.append(nc.dram_tensor("out_y", (B, T, D), F32, kind="ExternalOutput").ap())
    build(nc, *args)
    r = run_bass_kernel_spmd(nc, [arrays], core_ids=[0])
    return r.results[0]["out_y"]
```
